# Optimizing a Trainium2 kernel written in Bass

```python
import numpy as np
import jax
import jax.numpy as jnp

def _softmax(x, axis=-1):
    return jax.nn.softmax(x, axis=axis)

def _gelu(x):
    return jax.nn.gelu(x, approximate=True)

def _silu(x):
    return jax.nn.silu(x)

def _sigmoid(x):
    return jax.nn.sigmoid(x)

def _layernorm(x, axis=-1, eps=1e-05):
    m = jnp.mean(x, axis=axis, keepdims=True)
    v = jnp.var(x, axis=axis, keepdims=True)
    return (x - m) / jnp.sqrt(v + eps)

def _scatter_add(tgt, idx, src, axis=0):
    return tgt.at[idx].add(src)

def _segment_sum(src, seg, n):
    return jax.ops.segment_sum(src, seg, n)
kernel_name = 'mk_adj_resnorm_d1_adj_r2_5cf552'

def setup_inputs(seed: int=0):
    np.random.seed(seed)
    _w = jnp.asarray

    def _rec_inputs():
        import jax
        import jax.numpy as jnp
        _gk = jax.random.key(seed)
        x = 7.22e-05 + 1 * jax.random.normal(jax.random.fold_in(_gk, 1), (8, 1024, 512), jnp.float32)
        _a = jax.random.bernoulli(jax.random.fold_in(_gk, 2), 0.00390625, (1024, 1024))
        _a = jnp.logical_or(_a, jnp.eye(1024, dtype=bool))
        _af = _a.astype(jnp.float32)
        adj = _af
        return (x, adj)
    x, adj = _rec_inputs()

    def _L0_gnn_setup():
        import jax, jax.numpy as jnp
        import numpy as np
        EPS = 1e-08

        def _row_stochastic_causal(A, causal_mask):
            A = A * causal_mask
            deg = jnp.maximum(A.sum(axis=-1, keepdims=True), EPS)
            return A / deg
        key = jax.random.key(seed)
        k = jax.random.split(key, 5)
        B, N, D = (4, 1024, 512)
        s = 1.0 / np.sqrt(D)
        h = jax.random.normal(k[0], (B, N, D), dtype=jnp.float32)
        W_lang = jax.random.normal(k[1], (D, D), dtype=jnp.float32) * s
        W_grav = jax.random.normal(k[2], (D, D), dtype=jnp.float32) * s
        W_V = jax.random.normal(k[3], (D, D), dtype=jnp.float32) * s
        W_O = jax.random.normal(k[4], (D, D), dtype=jnp.float32) * s
        causal_mask = jnp.tril(jnp.ones((N, N), dtype=jnp.float32))
        gate_logit = jnp.zeros((), jnp.float32)
        log_sigma = jnp.zeros((), jnp.float32)
        return {'h': h, 'causal_mask': causal_mask, 'W_lang': W_lang, 'W_grav': W_grav, 'W_V': W_V, 'W_O': W_O, 'gate_logit': gate_logit, 'log_sigma': log_sigma}
    _L0_gnn_all = _L0_gnn_setup()
    _L0_gnn_in = {k: v for k, v in _L0_gnn_all.items() if k in ('W_lang', 'W_grav', 'W_V', 'W_O', 'gate_logit', 'log_sigma')}
    del _L0_gnn_all
    return {'x': x, 'adj': adj, 'L0_gnn_W_lang': _L0_gnn_in['W_lang'], 'L0_gnn_W_grav': _L0_gnn_in['W_grav'], 'L0_gnn_W_V': _L0_gnn_in['W_V'], 'L0_gnn_W_O': _L0_gnn_in['W_O'], 'L0_gnn_gate_logit': _L0_gnn_in['gate_logit'], 'L0_gnn_log_sigma': _L0_gnn_in['log_sigma']}

def reference(x, adj, L0_gnn_W_lang, L0_gnn_W_grav, L0_gnn_W_V, L0_gnn_W_O, L0_gnn_gate_logit, L0_gnn_log_sigma):
    import jax
    import jax.numpy as jnp

    def _L0_gnn_ref(h, causal_mask, W_lang, W_grav, W_V, W_O, gate_logit, log_sigma):
        import jax, jax.numpy as jnp
        import numpy as np
        EPS = 1e-08

        def _row_stochastic_causal(A, causal_mask):
            A = A * causal_mask
            deg = jnp.maximum(A.sum(axis=-1, keepdims=True), EPS)
            return A / deg
        z_l = jnp.einsum('bnd,ed->bne', h, W_lang)
        z_g = jnp.einsum('bnd,ed->bne', h, W_grav)
        v = jnp.einsum('bnd,ed->bne', h, W_V)
        N = h.shape[-2]
        not_eye = 1.0 - jnp.eye(N, dtype=h.dtype)
        zn = z_l / jnp.maximum(jnp.linalg.norm(z_l, axis=-1, keepdims=True), EPS)
        A_l = jnp.maximum(jnp.einsum('bnd,bmd->bnm', zn, zn), 0.0) * not_eye
        sq = jnp.sum(z_g * z_g, axis=-1, keepdims=True)
        d2 = jnp.maximum(sq + jnp.swapaxes(sq, -1, -2) - 2.0 * jnp.einsum('bnd,bmd->bnm', z_g, z_g), 0.0)
        sigma = jnp.exp(log_sigma)
        A_g = jnp.exp(-d2 / (2.0 * sigma * sigma)) * not_eye
        K_l = _row_stochastic_causal(A_l, causal_mask)
        K_g = _row_stochastic_causal(A_g, causal_mask)
        w_l = jax.nn.sigmoid(gate_logit)
        K = w_l * K_l + (1.0 - w_l) * K_g
        out = jnp.einsum('bnm,bmd->bnd', K, v)
        return jnp.einsum('bnd,ed->bne', out, W_O)
    x = _layernorm(x + _L0_gnn_ref(x, adj, L0_gnn_W_lang, L0_gnn_W_grav, L0_gnn_W_V, L0_gnn_W_O, L0_gnn_gate_logit, L0_gnn_log_sigma), axis=-1)
    return x

_drawn_inputs = setup_inputs


def setup_inputs(seed=0):
    import zlib

    import numpy as np

    out = dict(_drawn_inputs(seed))
    spreads = {}
    factors = {}
    for name, (base, spread) in spreads.items():
        noise = np.random.default_rng([zlib.crc32(name.encode()), seed]).standard_normal(out[name].shape)
        drawn = base * np.exp(spread * noise) if base else spread * noise
        out[name] = jnp.asarray(drawn.astype(out[name].dtype))
    for name, factor in factors.items():
        out[name] = (out[name] * factor).astype(out[name].dtype)
    return out
```

```python
from collections import namedtuple
from contextlib import ExitStack

import concourse.bass as bass
from concourse import mybir

P = 128
F32 = mybir.dt.float32
F16 = mybir.dt.float16
U32 = mybir.dt.uint32
ALU = mybir.AluOpType
ACT = mybir.ActivationFunctionType
AX_X = mybir.AxisListType.X
RMAX = bass.bass_isa.ReduceOp.max

EPS = 1e-8
LN_EPS = 1e-5
K_SCALE = 2.0 ** 13
EXPONENT = 0x7F800000
BANK = 512
HI, LO = 0, 1

Signal = namedtuple("Signal", "sem per_batch before")


def count(signal, b, n):
    assert signal.before + n > 0
    return b * signal.per_batch + (signal.before + n)


def program(nc, x, xT, adj, WlT, WgT, Wv, WoT, gate_logit, log_sigma, y):
    B, N, D = x.shape
    NT = N // P
    DC = D // P
    HALVES = N // BANK
    LAST = B - 1
    DMA = 16

    KEPT = NT // 2
    row_base = [sum(NT - 1 - r for r in range(i)) for i in range(KEPT + 1)]
    DIAG = row_base[KEPT]
    SLOTS = DIAG + NT

    def slot(i, j):
        return DIAG + i if i == j else row_base[i % KEPT] + j - i - 1

    BCAST_G, BCAST_L = 0, HALVES
    V_JOB = 2 * HALVES
    Z_JOB = V_JOB + NT
    Z_JOBS = 2 * DC * HALVES
    PROJ_JOBS = Z_JOB + Z_JOBS
    z_jobs = [(k, c, h) for h in range(HALVES) for k in range(2) for c in range(DC)]
    WVO_JOBS = DC

    def jobs(i, more):
        first, last = [(0, NT // 2), (NT // 2, NT), (0, 0), (0, 0)][i] if i < KEPT else (
            (2 * (i - KEPT), 2 * (i - KEPT) + 2) if i < NT else (Z_JOBS // 2, Z_JOBS))
        todo = [("v" if i < KEPT else "z", q) for q in range(first, last) if i < KEPT or more]
        mid = 0 if i < KEPT else 1 if i < NT else 2
        return todo[:mid], todo[mid:]

    def ring_index(job):
        return (V_JOB if job[0] == "v" else Z_JOB) + job[1]

    with ExitStack() as ctx:
        def sb(name, shape, dt=F32):
            return ctx.enter_context(nc.sbuf_tensor(name, shape, dt))

        def psum(name, shape):
            return ctx.enter_context(nc.psum_tensor(name, shape, F32))

        def signal(name, per_batch=0, before=0):
            return Signal(ctx.enter_context(nc.semaphore(name)), per_batch, before)

        gram = [psum("gram_l", [P, N]), psum("gram_g", [P, N])]
        proj = psum("proj", [P, 2, BANK])
        kt_ps = psum("kt_ps", [P, BANK])
        out_ps = psum("out_ps", [P, D])

        mask = sb("mask", [P, NT, N])
        wl = sb("wl", [P, 2, DC, D], F16)
        wg = sb("wg", [P, 2, DC, D], F16)
        wvo = sb("wvo", [P, 2, DC, D], F16)
        ident = sb("ident", [P, P])
        xT32 = sb("xT32", [P, DC, N])
        xs = sb("xs", [P, 2, DC, N], F16)
        z = [sb("zl", [P, 2, DC, N], F16), sb("zg", [P, 2, DC, N], F16)]
        vo = sb("vo", [P, 2, NT, D], F16)
        saved = [sb("saved_l", [P, SLOTS, P]), sb("saved_g", [P, SLOTS, P])]
        rn_b = sb("rn_b", [P, N])
        nsq_b = sb("nsq_b", [P, N])
        rmask = sb("rmask", [P, N])
        a_row = sb("a_row", [P, 2, N])
        e_row = sb("e_row", [P, 2, N])
        kt = sb("kt", [P, 2, NT, P], F16)
        xy = sb("xy", [P, 2, D])
        wmax = sb("wmax", [P, 8])
        wscale = sb("wscale", [P, 8])
        wtmp = sb("wtmp", [P, 8])
        gate = sb("gate", [P, 1])
        lsig = sb("lsig", [P, 1])
        gtmp = sb("gtmp", [P, 4])
        fixed = sb("fixed", [P, 4])
        xmax = sb("xmax", [P, DC + 2])
        sx = sb("sx", [P, 4])
        bc = sb("bc", [P, 8])
        sq = sb("sq", [P, 2, NT])
        norm = sb("norm", [P, NT])
        rn = sb("rn", [P, NT])
        nsq = sb("nsq", [P, NT])
        half = sb("half", [P, NT])
        mhalf = sb("mhalf", [P, 1])
        deg = sb("deg", [P, 2, 2])
        dinv = sb("dinv", [P, 2, 2])
        coef = sb("coef", [P, 2, 2])
        stats = sb("stats", [P, 6])
        mv = sb("mv", [P, 2, 2])
        lnp = sb("lnp", [P, 2, 4])

        w_loaded = [signal(f"w{n}_loaded") for n in range(4)]
        scalars_loaded = signal("scalars_loaded")
        mask_loaded = signal("mask_loaded")
        xT_loaded = signal("xT_loaded", DMA, DMA)
        x_loaded = [signal(f"x_loaded{s}", DMA * NT // 2) for s in range(2)]
        y_stored = [signal(f"y_stored{s}", DMA * NT // 2) for s in range(2)]
        gram_ready = [signal("gram_l_ready", NT + 1), signal("gram_g_ready", NT + 1)]
        proj_ready = signal("proj_ready", PROJ_JOBS, WVO_JOBS + Z_JOBS)
        kt_ready = signal("kt_ready", 2 * NT)
        out_ready = signal("out_ready", NT)
        gram_saved = [signal("gram_l_saved", NT), signal("gram_g_saved", NT)]
        w_hi = signal("w_hi")
        scalars_exp = signal("scalars_exp")
        x_hi = signal("x_hi", DC, DC)
        proj_hi = signal("proj_hi", NT + Z_JOBS, Z_JOBS)
        exp_done = signal("exp_done", NT)
        e_scaled = signal("e_scaled", NT)
        kt_hi = signal("kt_hi", 2 * NT)
        y_ready = signal("y_ready", NT)
        gram_drained = [signal("gram_l_drained", NT + 1, 1), signal("gram_g_drained", NT + 1, 1)]
        w_part = signal("w_part")
        w_scale_ready = signal("w_scale_ready")
        w_lo = signal("w_lo")
        wvo_part = signal("wvo_part")
        wvo_scale_ready = signal("wvo_scale_ready")
        wvo_lo = signal("wvo_lo")
        x_part = signal("x_part", 1, 1)
        x_scale_ready = signal("x_scale_ready", 1, 1)
        x_lo = signal("x_lo", DC, DC)
        sq_ready = signal("sq_ready", 1)
        rn_ready = signal("rn_ready", 1)
        nsq_ready = signal("nsq_ready", 1)
        proj_drained = signal("proj_drained", PROJ_JOBS, WVO_JOBS + Z_JOBS)
        coef_g_ready = signal("coef_g_ready", NT)
        k_formed = signal("k_formed", NT)
        kt_drained = signal("kt_drained", 2 * NT, 1)
        out_drained = signal("out_drained", NT, 1)
        mv_ready = signal("mv_ready", NT)
        VEC_SETUP = 17
        VEC_BATCH = 64
        vec_link = signal("vec_link", VEC_BATCH, VEC_SETUP)
        ident_zero = signal("ident_zero")
        ident_ready = signal("ident_ready")
        mask_ready = signal("mask_ready")
        halves_ready = signal("halves_ready")
        w_max_ready = signal("w_max_ready")
        wvo_max_ready = signal("wvo_max_ready")
        x_max_ready = signal("x_max_ready", 1, 1)
        norm_ready = signal("norm_ready", 1)
        rmask_ready = signal("rmask_ready", NT)
        ln_ready = signal("ln_ready", NT)
        pool_link = signal("pool_link", 2 * NT)
        passed = signal("passed")

        flat = lambda t, a: t[:].rearrange(a)
        w32 = [
            flat(saved[0], "p s q -> p (s q)")[:, 0:DC * D],
            flat(saved[1], "p s q -> p (s q)")[:, 0:DC * D],
            flat(a_row, "p s n -> p (s n)"),
            flat(vo, "p h t d -> p (h t d)").bitcast(F32)[:, 0:DC * D],
        ]
        wvo32 = flat(e_row, "p s n -> p (s n)")
        zg_flat = flat(z[1], "p h c n -> p (h c n)")
        wv_s = zg_flat[:, 0:2 * DC * D].rearrange("p (h c e) -> p h c e", h=2, c=DC)
        wo_s = zg_flat[:, 2 * DC * D:4 * DC * D].rearrange("p (h c e) -> p h c e", h=2, c=DC)
        w_split = [wl, wg, wv_s, wo_s]

        def split_of(w, part):
            return w[:, part, :, :].rearrange("p c e -> p (c e)")

        y_rows = y.rearrange("b (t p) d -> b t p d", p=P)
        x_rows = x.rearrange("b (t p) d -> b t p d", p=P)
        xT_rows = xT.rearrange("b (c p) n -> b p c n", p=P)
        x_wait = lambda r: DMA * (r // 2 + 1)

        block = ctx.enter_context(nc.Block())

        def hold(eng, signal, value):
            eng.wait_ge(signal.sem, value)
            eng.sem_inc(passed.sem, 1)

        @block.sync
        def _(sp):
            for n in (2, 3):
                src = (WlT, WgT, Wv, WoT)[n]
                sp.dma_start(w32[n].rearrange("p (c e) -> p c e", c=DC),
                             src.rearrange("(c p) e -> p c e", p=P)).then_inc(w_loaded[n].sem, DMA)
            sp.dma_start(xT32[:], xT_rows[0]).then_inc(xT_loaded.sem, DMA)
            for n in (0, 1):
                src = (WlT, WgT, Wv, WoT)[n]
                sp.dma_start(w32[n].rearrange("p (c e) -> p c e", c=DC),
                             src.rearrange("(c p) e -> p c e", p=P)).then_inc(w_loaded[n].sem, DMA)
            sp.dma_start(gate[:], gate_logit.broadcast_to([P, 1])).then_inc(scalars_loaded.sem, DMA)
            sp.dma_start(lsig[:], log_sigma.broadcast_to([P, 1])).then_inc(scalars_loaded.sem, DMA)
            sp.dma_start(mask[:], adj.rearrange("(t p) m -> p t m", p=P)).then_inc(mask_loaded.sem, DMA)

            def load_x(b, r):
                sp.dma_start(xy[:, r % 2, :], x_rows[b, r]).then_inc(x_loaded[r % 2].sem, DMA)

            def batch(b, more):
                if more:
                    sp.wait_ge(x_lo.sem, count(x_lo, b, 0))
                    sp.dma_start(xT32[:], xT_rows[b + 1]).then_inc(xT_loaded.sem, DMA)
                load_x(b, 0)
                load_x(b, 1)
                for r in range(NT):
                    sp.wait_ge(y_ready.sem, count(y_ready, b, r + 1))
                    sp.dma_start(y_rows[b, r], xy[:, r % 2, :]).then_inc(y_stored[r % 2].sem, DMA)
                    if r + 2 < NT:
                        sp.wait_ge(y_stored[r % 2].sem, count(y_stored[r % 2], b, x_wait(r)))
                        load_x(b, r + 2)
                for s in range(2):
                    hold(sp, y_stored[s], count(y_stored[s], b, x_wait(NT - 1)))

            with sp.Fori(0, LAST) as b:
                batch(b, True)
            batch(LAST, False)

        @block.tensor
        def _(pe):
            def three_passes(out, left, right, chunks, done=None):
                passes = [(c, a, b) for c in range(chunks) for a, b in ((HI, HI), (HI, LO), (LO, HI))]
                for n, (c, a, b) in enumerate(passes):
                    last = nc.tensor.matmul(out, left(a, c), right(b, c),
                                            start=(n == 0), stop=(n == len(passes) - 1))
                if done is not None:
                    last.then_inc(done.sem, 1)

            def ring_wait(b, n):
                k = count(proj_drained, b, n - 1)
                pe.wait_ge(proj_drained.sem, k)

            def z_job(b, q, n):
                k, c, h = z_jobs[q]
                w = (wl, wg)[k]
                ring_wait(b, n)
                three_passes(proj[:, n % 2, :], lambda a, d: w[:, a, d, c * P:(c + 1) * P],
                             lambda a, d: xs[:, a, d, h * BANK:(h + 1) * BANK], DC, proj_ready)

            def run_jobs(b, todo):
                for job in todo:
                    n = ring_index(job)
                    if job[0] == "v":
                        t = job[1]
                        ring_wait(b, n)
                        three_passes(proj[:, n % 2, :], lambda a, d: xs[:, a, d, t * P:(t + 1) * P],
                                     lambda a, d: wvo[:, a, d, :], DC, proj_ready)
                    else:
                        if job[1] == 0:
                            pe.wait_ge(x_lo.sem, count(x_lo, b, DC))
                        z_job(b, job[1], n)

            def diagonal(b, k):
                pe.wait_ge(gram_drained[k].sem, count(gram_drained[k], b, 0))
                for t in range(NT):
                    cols = slice(t * P, (t + 1) * P)
                    three_passes(gram[k][:, cols], lambda a, c: z[k][:, a, c, cols],
                                 lambda a, c: z[k][:, a, c, cols], DC,
                                 gram_ready[k] if t == NT - 1 else None)

            def gram_row(b, i, k):
                pe.wait_ge(gram_saved[k].sem, count(gram_saved[k], b, i + 1))
                for j in range(i + 1):
                    last = nc.tensor.transpose(gram[k][:, j * P:(j + 1) * P], saved[k][:, slot(j, i), :], ident[:])
                pieces = [(max((i + 1) * P, h * BANK), (h + 1) * BANK) for h in range(HALVES)]
                pieces = [(a, e) for a, e in pieces if a < e]
                for c in range(DC if pieces else 0):
                    for n, (l, r) in enumerate(((HI, HI), (HI, LO), (LO, HI))):
                        for a, e in pieces:
                            last = nc.tensor.matmul(gram[k][:, a:e], z[k][:, l, c, i * P:(i + 1) * P],
                                                    z[k][:, r, c, a:e], start=(c == 0 and n == 0),
                                                    stop=(c == DC - 1 and n == 2))
                last.then_inc(gram_ready[k].sem, 1)

            def spread(b, first, column, ready):
                pe.wait_ge(ready.sem, count(ready, b, 1))
                for h in range(HALVES):
                    ring_wait(b, first + h)
                    for t in range(BANK // P):
                        col = column[:, h * BANK // P + t:h * BANK // P + t + 1]
                        last = nc.tensor.transpose(proj[:, (first + h) % 2, t * P:(t + 1) * P],
                                                   col.broadcast_to([P, P]), ident[:])
                    last.then_inc(proj_ready.sem, 1)

            def turn_k(b, i, h):
                if h == 0:
                    pe.wait_ge(k_formed.sem, count(k_formed, b, i + 1))
                pe.wait_ge(kt_drained.sem, count(kt_drained, b, 2 * i + h))
                for t in range(NT // 2):
                    j = h * NT // 2 + t
                    last = nc.tensor.transpose(kt_ps[:, t * P:(t + 1) * P], a_row[:, i % 2, j * P:(j + 1) * P], ident[:])
                last.then_inc(kt_ready.sem, 1)

            def out_row(b, i):
                pe.wait_ge(out_drained.sem, count(out_drained, b, i))
                for j in range(NT):
                    if j % (NT // 2) == 0:
                        pe.wait_ge(kt_drained.sem, count(kt_drained, b, 2 * i + 1 + j // (NT // 2)))
                        if i == 0:
                            pe.wait_ge(proj_drained.sem, count(proj_drained, b, V_JOB + j + NT // 2))
                    for n, (l, r) in enumerate(((HI, HI), (HI, LO), (LO, HI))):
                        last = nc.tensor.matmul(out_ps[:], kt[:, l, j, :], vo[:, r, j, :],
                                                start=(j == 0 and n == 0), stop=(j == NT - 1 and n == 2))
                last.then_inc(out_ready.sem, 1)

            pe.wait_ge(w_lo.sem, 2)
            for i in range(WVO_JOBS):
                if i >= 2:
                    pe.wait_ge(proj_drained.sem, i - 1)
                three_passes(proj[:, i % 2, :], lambda a, c: wv_s[:, a, c, i * P:(i + 1) * P],
                             lambda a, c: wo_s[:, a, c, :], DC, proj_ready)
            pe.wait_ge(w_lo.sem, 4)
            pe.wait_ge(x_lo.sem, DC)
            for q in range(Z_JOBS):
                n = WVO_JOBS + q
                k, c, h = z_jobs[q]
                w = (wl, wg)[k]
                pe.wait_ge(proj_drained.sem, n - 1)
                three_passes(proj[:, n % 2, :], lambda a, d: w[:, a, d, c * P:(c + 1) * P],
                             lambda a, d: xs[:, a, d, h * BANK:(h + 1) * BANK], DC, proj_ready)
            pe.wait_ge(ident_ready.sem, 1)

            def batch(b, more):
                pe.wait_ge(proj_drained.sem, count(proj_drained, b, 0))
                diagonal(b, 1)
                diagonal(b, 0)
                for i in range(NT + 1):
                    before, after = jobs(i, more)
                    if i == 0:
                        spread(b, BCAST_G, nsq, nsq_ready)
                    else:
                        turn_k(b, i - 1, 0)
                    if i < NT:
                        gram_row(b, i, 1)
                    if i == 0:
                        spread(b, BCAST_L, rn, rn_ready)
                    run_jobs(b, before)
                    if i > 0:
                        turn_k(b, i - 1, 1)
                    if i < NT:
                        gram_row(b, i, 0)
                    run_jobs(b, after)
                    if i > 0:
                        out_row(b, i - 1)

            pe.wait_ge(wvo_lo.sem, 1)
            with pe.Fori(0, LAST) as b:
                batch(b, True)
            batch(LAST, False)

        @block.scalar
        def _(act):
            def split_hi(n):
                act.wait_ge(w_scale_ready.sem, 1 if n >= 2 else 2)
                nc.scalar.activation(split_of(w_split[n], HI), w32[n], ACT.Identity,
                                     scale=wscale[:, n:n + 1]).then_inc(w_hi.sem, 1)

            split_hi(2)
            split_hi(3)

            def x_chunk(c):
                nc.scalar.activation(xs[:, HI, c, :], xT32[:, c, :], ACT.Identity,
                                     scale=sx[:, 0:1]).then_inc(x_hi.sem, 1)

            act.wait_ge(x_scale_ready.sem, 1)
            for c in range(DC):
                x_chunk(c)
            split_hi(0)
            split_hi(1)
            act.wait_ge(scalars_loaded.sem, 2 * DMA)
            nc.scalar.activation(gtmp[:, 0:1], gate[:], ACT.Exp, scale=-1.0)
            nc.scalar.activation(gtmp[:, 1:2], lsig[:], ACT.Exp).then_inc(scalars_exp.sem, 1)

            def z_hi(q, slot_):
                k, c, h = z_jobs[q]
                nc.scalar.copy(z[k][:, HI, c, h * BANK:(h + 1) * BANK], proj[:, slot_, :]).then_inc(proj_hi.sem, 1)

            for q in range(Z_JOBS):
                n = WVO_JOBS + q
                act.wait_ge(proj_ready.sem, n + 1)
                z_hi(q, n % 2)
            act.wait_ge(wvo_scale_ready.sem, 1)
            nc.scalar.activation(split_of(wvo, HI), wvo32, ACT.Identity, scale=wscale[:, 4:5]).then_inc(w_hi.sem, 1)

            def run_jobs(b, todo):
                for job in todo:
                    n = ring_index(job)
                    act.wait_ge(proj_ready.sem, count(proj_ready, b, n + 1))
                    if job[0] == "v":
                        nc.scalar.copy(vo[:, HI, job[1], :], proj[:, n % 2, :]).then_inc(proj_hi.sem, 1)
                    else:
                        z_hi(job[1], n % 2)

            def save_row(b, i, k):
                act.wait_ge(gram_drained[k].sem, count(gram_drained[k], b, i + 2))
                s = slot(i, i + 1)
                nc.scalar.copy(saved[k][:, s:s + NT - 1 - i, :].rearrange("p s q -> p (s q)"),
                               gram[k][:, (i + 1) * P:]).then_inc(gram_saved[k].sem, 1)

            def turned(b, i, h):
                act.wait_ge(kt_ready.sem, count(kt_ready, b, 2 * i + h + 1))
                nc.scalar.copy(kt[:, HI, h * NT // 2:(h + 1) * NT // 2, :].rearrange("p t q -> p (t q)"),
                               kt_ps[:]).then_inc(kt_hi.sem, 1)

            def normalise(b, i):
                act.wait_ge(ln_ready.sem, count(ln_ready, b, i + 1))
                s = i % 2
                nc.scalar.activation(xy[:, s, :], xy[:, s, :], ACT.Identity, scale=lnp[:, s, 1:2],
                                     bias=lnp[:, s, 2:3]).then_inc(y_ready.sem, 1)

            def batch(b, more):
                for k in (1, 0):
                    act.wait_ge(gram_drained[k].sem, count(gram_drained[k], b, 1))
                    nc.scalar.copy(saved[k][:, DIAG:DIAG + NT, :].rearrange("p s q -> p (s q)"),
                                   gram[k][:]).then_inc(gram_saved[k].sem, 1)
                for i in range(NT + 1):
                    before, after = jobs(i, more)
                    if i > 0:
                        turned(b, i - 1, 0)
                    if i < NT:
                        act.wait_ge(gram_drained[1].sem, count(gram_drained[1], b, i + 2))
                        nc.scalar.activation(e_row[:, i % 2, :], e_row[:, i % 2, :], ACT.Exp,
                                             scale=bc[:, 3:4]).then_inc(exp_done.sem, 1)
                    if i < NT - 1:
                        save_row(b, i, 1)
                    run_jobs(b, before)
                    if i > 0:
                        turned(b, i - 1, 1)
                    if i < NT:
                        act.wait_ge(coef_g_ready.sem, count(coef_g_ready, b, i + 1))
                        nc.scalar.activation(e_row[:, i % 2, :], e_row[:, i % 2, :], ACT.Identity,
                                             scale=coef[:, i % 2, 1:2]).then_inc(e_scaled.sem, 1)
                    if i > 1:
                        normalise(b, i - 2)
                    if i < NT - 1:
                        save_row(b, i, 0)
                    run_jobs(b, after)
                    if more and i in (2, 3):
                        if i == 2:
                            act.wait_ge(x_scale_ready.sem, count(x_scale_ready, b, 1))
                            act.wait_ge(proj_ready.sem, count(proj_ready, b, Z_JOB))
                        for c in range((i - 2) * DC // 2, (i - 1) * DC // 2):
                            x_chunk(c)
                normalise(b, NT - 1)

            with act.Fori(0, LAST) as b:
                batch(b, True)
            batch(LAST, False)

        @block.vector
        def _(dve):
            links = [0]

            def link(ins, base):
                links[0] += 1
                ins.then_inc(vec_link.sem, 1)
                dve.wait_ge(vec_link.sem, base + links[0])

            def scale_from(out, top, tmp, base):
                link(nc.vector.tensor_scalar(tmp, top, 1e-30, None, ALU.max), base)
                link(nc.vector.tensor_scalar(tmp.bitcast(U32), tmp.bitcast(U32), EXPONENT, None, ALU.bitwise_and), base)
                link(nc.vector.reciprocal(tmp, tmp), base)
                return nc.vector.tensor_scalar(out, tmp, 4.0, None, ALU.mult)

            def top_of(out, in_):
                return nc.vector.tensor_reduce(out, in_, AX_X, ALU.max, apply_absolute_value=True)

            def split_lo(n):
                dve.wait_ge(w_hi.sem, {2: 1, 3: 2, 0: 3, 1: 4}[n])
                nc.vector.scalar_tensor_tensor(split_of(w_split[n], LO), w32[n], wscale[:, n:n + 1],
                                               split_of(w_split[n], HI), ALU.mult, ALU.subtract).then_inc(w_lo.sem, 1)

            for s in (gram_drained[0], gram_drained[1], kt_drained, out_drained):
                dve.sem_inc(s.sem, 1)
            for n in (2, 3):
                dve.wait_ge(w_loaded[n].sem, DMA)
                last = top_of(wmax[:, n:n + 1], w32[n])
            last.then_inc(w_part.sem, 1)
            dve.wait_ge(xT_loaded.sem, DMA)
            top_of(xmax[:, DC:DC + 1], xT32[:].rearrange("p c n -> p (c n)")).then_inc(x_part.sem, 1)
            dve.wait_ge(w_max_ready.sem, 1)
            scale_from(wscale[:, 2:4], wmax[:, 4:6], wtmp[:, 2:4], 0).then_inc(w_scale_ready.sem, 1)
            split_lo(2)
            split_lo(3)
            dve.wait_ge(x_max_ready.sem, 1)
            scale_from(sx[:, 0:1], xmax[:, DC + 1:DC + 2], sx[:, 1:2], 0).then_inc(x_scale_ready.sem, 1)

            def x_chunk(c, value):
                dve.wait_ge(x_hi.sem, value)
                nc.vector.scalar_tensor_tensor(xs[:, LO, c, :], xT32[:, c, :], sx[:, 0:1], xs[:, HI, c, :],
                                               ALU.mult, ALU.subtract).then_inc(x_lo.sem, 1)

            for c in range(DC):
                x_chunk(c, c + 1)
            for n in (0, 1):
                dve.wait_ge(w_loaded[n].sem, DMA)
                last = top_of(wmax[:, n:n + 1], w32[n])
            last.then_inc(w_part.sem, 1)
            for n in range(WVO_JOBS):
                dve.wait_ge(proj_ready.sem, n + 1)
                nc.vector.tensor_copy(wvo32[:, n * D:(n + 1) * D], proj[:, n % 2, :]).then_inc(proj_drained.sem, 1)
            dve.wait_ge(w_max_ready.sem, 2)
            scale_from(wscale[:, 0:2], wmax[:, 6:8], wtmp[:, 0:2], 0).then_inc(w_scale_ready.sem, 1)
            split_lo(0)
            split_lo(1)
            dve.wait_ge(proj_drained.sem, WVO_JOBS)
            top_of(wmax[:, 0:1], wvo32).then_inc(wvo_part.sem, 1)
            dve.wait_ge(scalars_exp.sem, 1)
            nc.vector.tensor_tensor(gtmp[:, 3:4], gtmp[:, 1:2], gtmp[:, 1:2], ALU.mult)
            link(nc.vector.tensor_scalar(gtmp[:, 2:3], gtmp[:, 0:1], 1.0, None, ALU.add), 0)
            link(nc.vector.reciprocal(gtmp[:, 2:4], gtmp[:, 2:4]), 0)
            nc.vector.tensor_scalar(fixed[:, 0:1], gtmp[:, 2:3], K_SCALE, None, ALU.mult)
            nc.vector.tensor_scalar(fixed[:, 1:2], gtmp[:, 2:3], -K_SCALE, K_SCALE, ALU.mult, ALU.add)
            link(nc.vector.tensor_copy(fixed[:, 2:3], gtmp[:, 3:4]), 0)

            def z_lo(q, s):
                k, c, h = z_jobs[q]
                cols = slice(h * BANK, (h + 1) * BANK)
                nc.vector.tensor_tensor(z[k][:, LO, c, cols], proj[:, s, :], z[k][:, HI, c, cols],
                                        ALU.subtract).then_inc(proj_drained.sem, 1)

            for q in range(Z_JOBS):
                dve.wait_ge(proj_hi.sem, q + 1)
                z_lo(q, (WVO_JOBS + q) % 2)
            dve.wait_ge(wvo_max_ready.sem, 1)
            scale_from(wscale[:, 4:5], wmax[:, 1:2], wtmp[:, 4:5], 0).then_inc(wvo_scale_ready.sem, 1)
            dve.wait_ge(wvo_scale_ready.sem, 1)
            link(nc.vector.tensor_scalar(wtmp[:, 5:6], wscale[:, 4:5], wscale[:, 2:3], wscale[:, 3:4],
                                         ALU.mult, ALU.mult), 0)
            link(nc.vector.tensor_copy(fixed[:, 3:4], wtmp[:, 5:6]), 0)
            dve.wait_ge(w_hi.sem, 5)
            nc.vector.scalar_tensor_tensor(split_of(wvo, LO), wvo32, wscale[:, 4:5], split_of(wvo, HI),
                                           ALU.mult, ALU.subtract).then_inc(wvo_lo.sem, 1)
            assert links[0] == VEC_SETUP, links
            dve.wait_ge(wvo_lo.sem, 1)
            dve.wait_ge(ident_ready.sem, 1)
            dve.wait_ge(mask_ready.sem, 1)

            def run_jobs(b, todo):
                for job in todo:
                    n = ring_index(job)
                    dve.wait_ge(proj_hi.sem, count(proj_hi, b, n - V_JOB + 1))
                    if job[0] == "v":
                        t = job[1]
                        nc.vector.tensor_tensor(vo[:, LO, t, :], proj[:, n % 2, :], vo[:, HI, t, :],
                                                ALU.subtract).then_inc(proj_drained.sem, 1)
                    else:
                        z_lo(job[1], n % 2)

            def squares(b, k, done):
                dve.wait_ge(gram_ready[k].sem, count(gram_ready[k], b, 1))
                prod = e_row[:, k, :].rearrange("p (t q) -> p t q", t=NT)
                eye = ident[:].unsqueeze(1).broadcast_to([P, NT, P])
                nc.vector.tensor_tensor(prod, gram[k][:].rearrange("p (t q) -> p t q", t=NT), eye,
                                        ALU.mult).then_inc(gram_drained[k].sem, 1)
                dve.wait_ge(gram_drained[k].sem, count(gram_drained[k], b, 1))
                last = nc.vector.tensor_reduce(sq[:, k, :], prod, AX_X, ALU.add)
                if done is not None:
                    last.then_inc(done.sem, 1)
                return last

            def unspread(b, first, to):
                for h in range(HALVES):
                    n = first + h
                    dve.wait_ge(proj_ready.sem, count(proj_ready, b, n + 1))
                    nc.vector.tensor_copy(to[:, h * BANK:(h + 1) * BANK], proj[:, n % 2, :]).then_inc(proj_drained.sem, 1)

            def turned(b, i, h):
                dve.wait_ge(kt_hi.sem, count(kt_hi, b, 2 * i + h + 1))
                part = lambda s: kt[:, s, h * NT // 2:(h + 1) * NT // 2, :].rearrange("p t q -> p (t q)")
                nc.vector.tensor_tensor(part(LO), kt_ps[:], part(HI), ALU.subtract).then_inc(kt_drained.sem, 1)

            def residual(b, i, base):
                s = i % 2
                dve.wait_ge(out_ready.sem, count(out_ready, b, i + 1))
                dve.wait_ge(x_loaded[s].sem, count(x_loaded[s], b, x_wait(i)))
                nc.vector.scalar_tensor_tensor(xy[:, s, :], out_ps[:], bc[:, 4:5], xy[:, s, :],
                                               ALU.mult, ALU.add).then_inc(out_drained.sem, 1)
                dve.wait_ge(out_drained.sem, count(out_drained, b, i + 1))
                links[0] += 1
                nc.vector.bn_stats(stats[:], xy[:, s, :]).then_inc(vec_link.sem, 1)
                hold(dve, vec_link, base + links[0])
                nc.vector.bn_aggr(mv[:, s, :], stats[:]).then_inc(mv_ready.sem, 1)

            def batch(b, more):
                base = count(vec_link, b, 0)
                links[0] = 0
                link(squares(b, 1, None), base)
                nc.vector.tensor_scalar(nsq[:], sq[:, 1, :], -0.5, None, ALU.mult).then_inc(nsq_ready.sem, 1)
                nc.vector.tensor_tensor(bc[:, 0:1], sx[:, 0:1], wscale[:, 0:1], ALU.mult)
                nc.vector.tensor_tensor(bc[:, 1:2], sx[:, 0:1], wscale[:, 1:2], ALU.mult)
                link(nc.vector.tensor_tensor(bc[:, 2:3], sx[:, 0:1], fixed[:, 3:4], ALU.mult), base)
                nc.vector.tensor_scalar(bc[:, 5:6], bc[:, 0:1], EPS, None, ALU.mult)
                link(nc.vector.reciprocal(bc[:, 6:8], bc[:, 1:3]), base)
                nc.vector.tensor_scalar(bc[:, 4:5], bc[:, 7:8], 1.0 / K_SCALE, None, ALU.mult)
                nc.vector.tensor_scalar(bc[:, 3:4], bc[:, 6:7], bc[:, 6:7], fixed[:, 2:3],
                                        ALU.mult, ALU.mult)
                dve.wait_ge(nsq_ready.sem, count(nsq_ready, b, 1))
                squares(b, 0, sq_ready)
                unspread(b, BCAST_G, nsq_b)
                dve.wait_ge(norm_ready.sem, count(norm_ready, b, 1))
                link(nc.vector.tensor_scalar(norm[:], norm[:], bc[:, 5:6], None, ALU.max), base)
                nc.vector.reciprocal(rn[:], norm[:]).then_inc(rn_ready.sem, 1)
                dve.wait_ge(rn_ready.sem, count(rn_ready, b, 1))
                dve.wait_ge(proj_drained.sem, count(proj_drained, b, BCAST_G + HALVES))

                for i in range(NT + 1):
                    s = i % 2
                    before, after = jobs(i, more)
                    if i > 0:
                        turned(b, i - 1, 0)
                    if i > 1:
                        residual(b, i - 2, base)
                    if i < NT:
                        dve.wait_ge(gram_ready[1].sem, count(gram_ready[1], b, i + 2))
                        nc.vector.scalar_tensor_tensor(e_row[:, s, :], gram[1][:], nsq[:, i:i + 1], nsq_b[:],
                                                       ALU.add, ALU.add).then_inc(gram_drained[1].sem, 1)
                    if i == 0:
                        unspread(b, BCAST_L, rn_b)
                    if i < NT:
                        dve.wait_ge(exp_done.sem, count(exp_done, b, i + 1))
                        link(nc.vector.scalar_tensor_tensor(e_row[:, s, :], e_row[:, s, :], 1.0, mask[:, i, :],
                                                            ALU.min, ALU.mult, accum_out=deg[:, s, 1:2]), base)
                        link(nc.vector.tensor_scalar(dinv[:, s, 1:2], deg[:, s, 1:2], EPS, None, ALU.max), base)
                        link(nc.vector.reciprocal(dinv[:, s, 1:2], dinv[:, s, 1:2]), base)
                        nc.vector.tensor_scalar(coef[:, s, 1:2], dinv[:, s, 1:2], fixed[:, 1:2], None,
                                                ALU.mult).then_inc(coef_g_ready.sem, 1)
                    run_jobs(b, before)
                    if i > 0:
                        turned(b, i - 1, 1)
                    if i < NT:
                        dve.wait_ge(rmask_ready.sem, count(rmask_ready, b, i + 1))
                        dve.wait_ge(gram_ready[0].sem, count(gram_ready[0], b, i + 2))
                        nc.vector.scalar_tensor_tensor(a_row[:, s, :], gram[0][:], 0.0, rmask[:], ALU.max, ALU.mult,
                                                       accum_out=deg[:, s, 0:1]).then_inc(gram_drained[0].sem, 1)
                        dve.wait_ge(gram_drained[0].sem, count(gram_drained[0], b, i + 2))
                        link(nc.vector.tensor_scalar(dinv[:, s, 0:1], deg[:, s, 0:1], rn[:, i:i + 1], EPS,
                                                     ALU.mult, ALU.max), base)
                        link(nc.vector.reciprocal(dinv[:, s, 0:1], dinv[:, s, 0:1]), base)
                        link(nc.vector.tensor_scalar(coef[:, s, 0:1], dinv[:, s, 0:1], rn[:, i:i + 1], fixed[:, 0:1],
                                                     ALU.mult, ALU.mult), base)
                        dve.wait_ge(e_scaled.sem, count(e_scaled, b, i + 1))
                        nc.vector.scalar_tensor_tensor(a_row[:, s, :], a_row[:, s, :], coef[:, s, 0:1], e_row[:, s, :],
                                                       ALU.mult, ALU.add).then_inc(k_formed.sem, 1)
                    run_jobs(b, after)
                    if more and i in (0, 1):
                        if i == 0:
                            dve.wait_ge(xT_loaded.sem, count(xT_loaded, b, DMA))
                        part = slice(i * DC // 2, (i + 1) * DC // 2)
                        last = top_of(xmax[:, part], xT32[:, part, :])
                        if i == 1:
                            link(last, base)
                            nc.vector.tensor_reduce(xmax[:, DC:DC + 1], xmax[:, 0:DC], AX_X,
                                                    ALU.max).then_inc(x_part.sem, 1)
                    if more and i in (2, 3):
                        if i == 2:
                            dve.wait_ge(x_max_ready.sem, count(x_max_ready, b, 1))
                            scale_from(sx[:, 0:1], xmax[:, DC + 1:DC + 2], sx[:, 1:2], base).then_inc(x_scale_ready.sem, 1)
                        for c in range((i - 2) * DC // 2, (i - 1) * DC // 2):
                            x_chunk(c, count(x_hi, b, c + 1))
                residual(b, NT - 1, base)
                return links[0]

            with dve.Fori(0, LAST) as b:
                used = batch(b, True)
            assert used == vec_link.per_batch, used
            batch(LAST, False)

        @block.gpsimd
        def _(pool):
            nc.gpsimd.memset(ident[:], 0.0).then_inc(ident_zero.sem, 1)
            nc.gpsimd.memset(half[:], 0.5)
            nc.gpsimd.memset(mhalf[:], -0.5).then_inc(halves_ready.sem, 1)
            pool.wait_ge(ident_zero.sem, 1)
            nc.gpsimd.affine_select(out=ident[:], in_=ident[:], compare_op=ALU.not_equal, fill=1.0, base=0,
                                    pattern=[[-1, P]], channel_multiplier=1).then_inc(ident_ready.sem, 1)
            pool.wait_ge(w_part.sem, 1)
            nc.gpsimd.partition_all_reduce(wmax[:, 4:6], wmax[:, 2:4], P, RMAX).then_inc(w_max_ready.sem, 1)
            pool.wait_ge(x_part.sem, 1)
            nc.gpsimd.partition_all_reduce(xmax[:, DC + 1:DC + 2], xmax[:, DC:DC + 1], P, RMAX).then_inc(x_max_ready.sem, 1)
            pool.wait_ge(w_part.sem, 2)
            nc.gpsimd.partition_all_reduce(wmax[:, 6:8], wmax[:, 0:2], P, RMAX).then_inc(w_max_ready.sem, 1)
            pool.wait_ge(mask_loaded.sem, DMA)
            for t in range(NT):
                tile = mask[:, t, t * P:(t + 1) * P]
                last = nc.gpsimd.affine_select(out=tile, in_=tile, compare_op=ALU.not_equal, fill=0.0, base=0,
                                               pattern=[[-1, P]], channel_multiplier=1)
            last.then_inc(mask_ready.sem, 1)
            pool.wait_ge(wvo_part.sem, 1)
            nc.gpsimd.partition_all_reduce(wmax[:, 1:2], wmax[:, 0:1], P, RMAX).then_inc(wvo_max_ready.sem, 1)
            pool.wait_ge(halves_ready.sem, 1)
            pool.wait_ge(mask_ready.sem, 1)

            def masked_norms(b, i):
                if i == 0:
                    pool.wait_ge(proj_drained.sem, count(proj_drained, b, BCAST_L + HALVES))
                pool.wait_ge(gram_drained[0].sem, count(gram_drained[0], b, i + 1))
                nc.gpsimd.tensor_tensor(rmask[:], mask[:, i, :], rn_b[:], ALU.mult).then_inc(rmask_ready.sem, 1)

            def layer_norm(b, i):
                s = i % 2
                hold(pool, mv_ready, count(mv_ready, b, i + 1))
                nc.gpsimd.tensor_scalar(lnp[:, s, 0:1], mv[:, s, 1:2], LN_EPS, 1.0, ALU.add,
                                        ALU.mult).then_inc(pool_link.sem, 1)
                pool.wait_ge(pool_link.sem, count(pool_link, b, 2 * i + 1))
                nc.gpsimd.tensor_tensor(lnp[:, s, 1:2], lnp[:, s, 0:1], mhalf[:], ALU.pow).then_inc(pool_link.sem, 1)
                hold(pool, pool_link, count(pool_link, b, 2 * i + 2))
                nc.gpsimd.tensor_scalar(lnp[:, s, 2:3], mv[:, s, 0:1], lnp[:, s, 1:2], -1.0, ALU.mult,
                                        ALU.mult).then_inc(ln_ready.sem, 1)

            def batch(b, more):
                pool.wait_ge(sq_ready.sem, count(sq_ready, b, 1))
                nc.gpsimd.tensor_tensor(norm[:], sq[:, 0, :], half[:], ALU.pow).then_inc(norm_ready.sem, 1)
                masked_norms(b, 0)
                for i in range(NT + 1):
                    if i + 1 < NT:
                        masked_norms(b, i + 1)
                    if more and i == 1:
                        hold(pool, x_part, count(x_part, b, 1))
                        nc.gpsimd.partition_all_reduce(xmax[:, DC + 1:DC + 2], xmax[:, DC:DC + 1], P,
                                                       RMAX).then_inc(x_max_ready.sem, 1)
                    if i > 1:
                        layer_norm(b, i - 2)
                layer_norm(b, NT - 1)

            with pool.Fori(0, LAST) as b:
                batch(b, True)
            batch(LAST, False)


def kernel(x, adj, L0_gnn_W_lang, L0_gnn_W_grav, L0_gnn_W_V, L0_gnn_W_O, L0_gnn_gate_logit, L0_gnn_log_sigma):
    import numpy as np
    import concourse.bacc as bacc
    from concourse.bass_utils import run_bass_kernel_spmd

    x = np.asarray(x)
    arrays = {
        "x": np.ascontiguousarray(x),
        "xT": np.ascontiguousarray(x.transpose(0, 2, 1)),
        "adj": np.ascontiguousarray(adj),
        "WlT": np.ascontiguousarray(np.asarray(L0_gnn_W_lang).T),
        "WgT": np.ascontiguousarray(np.asarray(L0_gnn_W_grav).T),
        "Wv": np.ascontiguousarray(L0_gnn_W_V),
        "WoT": np.ascontiguousarray(np.asarray(L0_gnn_W_O).T),
        "gate_logit": np.asarray(L0_gnn_gate_logit).reshape(1, 1),
        "log_sigma": np.asarray(L0_gnn_log_sigma).reshape(1, 1),
    }
    nc = bacc.Bacc("TRN2", target_bir_lowering=False, num_devices=1)
    args = [nc.dram_tensor(n, a.shape, mybir.dt.from_np(a.dtype), kind="ExternalInput").ap() for n, a in arrays.items()]
    out = nc.dram_tensor("y", x.shape, F32, kind="ExternalOutput").ap()
    program(nc, *args, out)
    r = run_bass_kernel_spmd(nc, [arrays], core_ids=[0])
    return r.results[0]["y"]
```

```python
from collections import namedtuple
from contextlib import ExitStack

import concourse.bass as bass
from concourse import mybir

P = 128
F32 = mybir.dt.float32
F16 = mybir.dt.float16
U32 = mybir.dt.uint32
ALU = mybir.AluOpType
ACT = mybir.ActivationFunctionType
AX_X = mybir.AxisListType.X
RMAX = bass.bass_isa.ReduceOp.max

EPS = 1e-8
LN_EPS = 1e-5
K_SCALE = 2.0 ** 13
EXPONENT = 0x7F800000
BANK = 512
HI, LO = 0, 1

Signal = namedtuple("Signal", "sem per_batch before")


def count(signal, b, n):
    assert signal.before + n > 0
    return b * signal.per_batch + (signal.before + n)


def program(nc, x, xT, adj, WlT, WgT, Wv, WoT, gate_logit, log_sigma, y):
    B, N, D = x.shape
    NT = N // P
    DC = D // P
    HALVES = N // BANK
    LAST = B - 1
    DMA = 16

    KEPT = NT // 2
    row_base = [sum(NT - 1 - r for r in range(i)) for i in range(KEPT + 1)]
    DIAG = row_base[KEPT]
    SLOTS = DIAG + NT

    def slot(i, j):
        return DIAG + i if i == j else row_base[i % KEPT] + j - i - 1

    BCAST_G, BCAST_L = 0, HALVES
    V_JOB = 2 * HALVES
    Z_JOB = V_JOB + NT
    Z_JOBS = 2 * DC * HALVES
    PROJ_JOBS = Z_JOB + Z_JOBS
    z_jobs = [(k, c, h) for h in range(HALVES) for k in range(2) for c in range(DC)]
    WVO_JOBS = DC
    of_kind = [[("z", q) for q, job in enumerate(z_jobs) if job[0] == k] for k in range(2)]
    setup_jobs = of_kind[0] + [("wvo", i) for i in range(WVO_JOBS)] + of_kind[1]

    def jobs(i, more):
        first, last = [(0, NT // 2), (NT // 2, NT), (0, 0), (0, 0)][i] if i < KEPT else (
            (2 * (i - KEPT), 2 * (i - KEPT) + 2) if i < NT else (Z_JOBS // 2, Z_JOBS))
        todo = [("v" if i < KEPT else "z", q) for q in range(first, last) if i < KEPT or more]
        mid = 0 if i < KEPT else 1 if i < NT else 2
        return todo[:mid], todo[mid:]

    def turn_early(i, more):
        return not more and i >= 3

    def ring_index(job):
        return (V_JOB if job[0] == "v" else Z_JOB) + job[1]

    with ExitStack() as ctx:
        def sb(name, shape, dt=F32):
            return ctx.enter_context(nc.sbuf_tensor(name, shape, dt))

        def psum(name, shape):
            return ctx.enter_context(nc.psum_tensor(name, shape, F32))

        def signal(name, per_batch=0, before=0):
            return Signal(ctx.enter_context(nc.semaphore(name)), per_batch, before)

        gram = [psum("gram_l", [P, N]), psum("gram_g", [P, N])]
        proj = psum("proj", [P, 2, BANK])
        kt_ps = psum("kt_ps", [P, BANK])
        out_ps = psum("out_ps", [P, D])

        mask = sb("mask", [P, NT, N])
        wl = sb("wl", [P, 2, DC, D], F16)
        wg = sb("wg", [P, 2, DC, D], F16)
        wvo = sb("wvo", [P, 2, DC, D], F16)
        ident = sb("ident", [P, P])
        xT32 = sb("xT32", [P, DC, N])
        xs = sb("xs", [P, 2, DC, N], F16)
        z = [sb("zl", [P, 2, DC, N], F16), sb("zg", [P, 2, DC, N], F16)]
        vo = sb("vo", [P, 2, NT, D], F16)
        saved = [sb("saved_l", [P, SLOTS, P]), sb("saved_g", [P, SLOTS, P])]
        rn_b = sb("rn_b", [P, N])
        nsq_b = sb("nsq_b", [P, N])
        rmask = sb("rmask", [P, N])
        a_row = sb("a_row", [P, 2, N])
        e_row = sb("e_row", [P, 2, N])
        kt = sb("kt", [P, 2, NT, P], F16)
        xy = sb("xy", [P, 2, D])
        wmax = sb("wmax", [P, 5])
        wtop = sb("wtop", [P, 5])
        wscale = sb("wscale", [P, 5])
        wtmp = sb("wtmp", [P, 6])
        gate = sb("gate", [P, 1])
        lsig = sb("lsig", [P, 1])
        gtmp = sb("gtmp", [P, 4])
        fixed = sb("fixed", [P, 4])
        xmax = sb("xmax", [P, DC + 2])
        sx = sb("sx", [P, 4])
        bc = sb("bc", [P, 8])
        sq = sb("sq", [P, 2, NT])
        norm = sb("norm", [P, NT])
        rn = sb("rn", [P, NT])
        nsq = sb("nsq", [P, NT])
        half = sb("half", [P, NT])
        mhalf = sb("mhalf", [P, 1])
        deg = sb("deg", [P, 2, 2])
        dinv = sb("dinv", [P, 2, 2])
        coef = sb("coef", [P, 2, 2])
        stats = sb("stats", [P, 6])
        mv = sb("mv", [P, 2, 2])
        lnp = sb("lnp", [P, 2, 4])

        w_loaded = [signal(f"w{n}_loaded") for n in range(4)]
        scalars_loaded = signal("scalars_loaded")
        mask_loaded = signal("mask_loaded")
        first_xT_loaded = [signal(f"first_xT{c}_loaded") for c in range(DC)]
        xT_loaded = signal("xT_loaded", DMA)
        x_loaded = [signal(f"x_loaded{s}", DMA * NT // 2) for s in range(2)]
        y_stored = [signal(f"y_stored{s}", DMA * NT // 2) for s in range(2)]
        gram_ready = [signal("gram_l_ready", NT + 1), signal("gram_g_ready", NT + 1)]
        proj_ready = signal("proj_ready", PROJ_JOBS, WVO_JOBS + Z_JOBS)
        kt_ready = signal("kt_ready", 2 * NT)
        out_ready = signal("out_ready", NT)
        gram_saved = [signal("gram_l_saved", NT), signal("gram_g_saved", NT)]
        w_hi = signal("w_hi")
        scalars_exp = signal("scalars_exp")
        x_hi = signal("x_hi", DC, DC)
        proj_hi = signal("proj_hi", NT + Z_JOBS, Z_JOBS)
        exp_done = signal("exp_done", NT)
        e_scaled = signal("e_scaled", NT)
        kt_hi = signal("kt_hi", 2 * NT)
        y_ready = signal("y_ready", NT)
        gram_drained = [signal("gram_l_drained", NT + 1, 1), signal("gram_g_drained", NT + 1, 1)]
        w_part = signal("w_part")
        w_scale_ready = signal("w_scale_ready")
        w_lo = signal("w_lo")
        x_part = signal("x_part", 1, 1)
        x_scale_ready = signal("x_scale_ready", 1, 1)
        x_lo = signal("x_lo", DC, DC)
        sq_ready = signal("sq_ready", 1)
        rn_ready = signal("rn_ready", 1)
        nsq_ready = signal("nsq_ready", 1)
        proj_drained = signal("proj_drained", PROJ_JOBS, WVO_JOBS + Z_JOBS)
        coef_g_ready = signal("coef_g_ready", NT)
        k_formed = signal("k_formed", NT)
        kt_drained = signal("kt_drained", 2 * NT, 1)
        out_drained = signal("out_drained", NT, 1)
        mv_ready = signal("mv_ready", NT)
        VEC_SETUP = 18
        VEC_BATCH = 64
        vec_link = signal("vec_link", VEC_BATCH, VEC_SETUP)
        ident_zero = signal("ident_zero")
        ident_ready = signal("ident_ready")
        mask_ready = signal("mask_ready")
        halves_ready = signal("halves_ready")
        w_max_ready = signal("w_max_ready")
        x_max_ready = signal("x_max_ready", 1, 1)
        norm_ready = signal("norm_ready", 1)
        rmask_ready = signal("rmask_ready", NT)
        ln_ready = signal("ln_ready", NT)
        pool_link = signal("pool_link", 2 * NT)
        passed = signal("passed")

        flat = lambda t, a: t[:].rearrange(a)
        w32 = [
            flat(saved[0], "p s q -> p (s q)")[:, 0:DC * D],
            flat(saved[1], "p s q -> p (s q)")[:, 0:DC * D],
            flat(a_row, "p s n -> p (s n)"),
            flat(vo, "p h t d -> p (h t d)").bitcast(F32)[:, 0:DC * D],
        ]
        wvo32 = flat(e_row, "p s n -> p (s n)")
        w32.append(wvo32)
        zg_flat = flat(z[1], "p h c n -> p (h c n)")
        wv_s = zg_flat[:, 0:2 * DC * D].rearrange("p (h c e) -> p h c e", h=2, c=DC)
        wo_s = zg_flat[:, 2 * DC * D:4 * DC * D].rearrange("p (h c e) -> p h c e", h=2, c=DC)
        w_split = [wl, wg, wv_s, wo_s, wvo]

        def split_of(w, part):
            return w[:, part, :, :].rearrange("p c e -> p (c e)")

        y_rows = y.rearrange("b (t p) d -> b t p d", p=P)
        x_rows = x.rearrange("b (t p) d -> b t p d", p=P)
        xT_rows = xT.rearrange("b (c p) n -> b p c n", p=P)
        x_wait = lambda r: DMA * (r // 2 + 1)

        block = ctx.enter_context(nc.Block())

        def own_bank(b, i):
            return isinstance(b, int) and turn_early(i + 1, b < LAST)

        def kt_bank(b, i, h):
            return proj[:, 0, :] if h == 1 and own_bank(b, i) else kt_ps[:]

        def hold(eng, signal, value):
            eng.wait_ge(signal.sem, value)
            eng.sem_inc(passed.sem, 1)

        @block.sync
        def _(sp):
            for c in range(DC):
                sp.dma_start(xT32[:, c, :], xT_rows[0][:, c, :]).then_inc(first_xT_loaded[c].sem, DMA)
            for n, src in enumerate((WlT, WgT, Wv, WoT)):
                sp.dma_start(w32[n].rearrange("p (c e) -> p c e", c=DC),
                             src.rearrange("(c p) e -> p c e", p=P)).then_inc(w_loaded[n].sem, DMA)
            sp.dma_start(gate[:], gate_logit.broadcast_to([P, 1])).then_inc(scalars_loaded.sem, DMA)
            sp.dma_start(lsig[:], log_sigma.broadcast_to([P, 1])).then_inc(scalars_loaded.sem, DMA)
            sp.dma_start(mask[:], adj.rearrange("(t p) m -> p t m", p=P)).then_inc(mask_loaded.sem, DMA)

            def load_x(b, r):
                sp.dma_start(xy[:, r % 2, :], x_rows[b, r]).then_inc(x_loaded[r % 2].sem, DMA)

            def batch(b, more):
                if more:
                    sp.wait_ge(x_lo.sem, count(x_lo, b, 0))
                    sp.dma_start(xT32[:], xT_rows[b + 1]).then_inc(xT_loaded.sem, DMA)
                load_x(b, 0)
                load_x(b, 1)
                for r in range(NT):
                    sp.wait_ge(y_ready.sem, count(y_ready, b, r + 1))
                    sp.dma_start(y_rows[b, r], xy[:, r % 2, :]).then_inc(y_stored[r % 2].sem, DMA)
                    if r + 2 < NT:
                        sp.wait_ge(y_stored[r % 2].sem, count(y_stored[r % 2], b, x_wait(r)))
                        load_x(b, r + 2)
                for s in range(2):
                    hold(sp, y_stored[s], count(y_stored[s], b, x_wait(NT - 1)))

            with sp.Fori(0, LAST) as b:
                batch(b, True)
            batch(LAST, False)

        @block.tensor
        def _(pe):
            def three_passes(out, left, right, chunks, done=None):
                passes = [(c, a, b) for c in range(chunks) for a, b in ((HI, HI), (HI, LO), (LO, HI))]
                for n, (c, a, b) in enumerate(passes):
                    last = nc.tensor.matmul(out, left(a, c), right(b, c),
                                            start=(n == 0), stop=(n == len(passes) - 1))
                if done is not None:
                    last.then_inc(done.sem, 1)

            def ring_wait(b, n):
                k = count(proj_drained, b, n - 1)
                pe.wait_ge(proj_drained.sem, k)

            def z_job(b, q, n):
                k, c, h = z_jobs[q]
                w = (wl, wg)[k]
                ring_wait(b, n)
                three_passes(proj[:, n % 2, :], lambda a, d: w[:, a, d, c * P:(c + 1) * P],
                             lambda a, d: xs[:, a, d, h * BANK:(h + 1) * BANK], DC, proj_ready)

            def run_jobs(b, todo):
                for job in todo:
                    n = ring_index(job)
                    if job[0] == "v":
                        t = job[1]
                        ring_wait(b, n)
                        three_passes(proj[:, n % 2, :], lambda a, d: xs[:, a, d, t * P:(t + 1) * P],
                                     lambda a, d: wvo[:, a, d, :], DC, proj_ready)
                    else:
                        if job[1] == 0:
                            pe.wait_ge(x_lo.sem, count(x_lo, b, DC))
                        z_job(b, job[1], n)

            def diagonal(b, k):
                pe.wait_ge(gram_drained[k].sem, count(gram_drained[k], b, 0))
                for t in range(NT):
                    cols = slice(t * P, (t + 1) * P)
                    three_passes(gram[k][:, cols], lambda a, c: z[k][:, a, c, cols],
                                 lambda a, c: z[k][:, a, c, cols], DC,
                                 gram_ready[k] if t == NT - 1 else None)

            def gram_row(b, i, k):
                pe.wait_ge(gram_saved[k].sem, count(gram_saved[k], b, i + 1))
                for j in range(i + 1):
                    last = nc.tensor.transpose(gram[k][:, j * P:(j + 1) * P], saved[k][:, slot(j, i), :], ident[:])
                pieces = [(max((i + 1) * P, h * BANK), (h + 1) * BANK) for h in range(HALVES)]
                pieces = [(a, e) for a, e in pieces if a < e]
                for c in range(DC if pieces else 0):
                    for n, (l, r) in enumerate(((HI, HI), (HI, LO), (LO, HI))):
                        for a, e in pieces:
                            last = nc.tensor.matmul(gram[k][:, a:e], z[k][:, l, c, i * P:(i + 1) * P],
                                                    z[k][:, r, c, a:e], start=(c == 0 and n == 0),
                                                    stop=(c == DC - 1 and n == 2))
                last.then_inc(gram_ready[k].sem, 1)

            def spread(b, first, column, ready):
                pe.wait_ge(ready.sem, count(ready, b, 1))
                for h in range(HALVES):
                    ring_wait(b, first + h)
                    for t in range(BANK // P):
                        col = column[:, h * BANK // P + t:h * BANK // P + t + 1]
                        last = nc.tensor.transpose(proj[:, (first + h) % 2, t * P:(t + 1) * P],
                                                   col.broadcast_to([P, P]), ident[:])
                    last.then_inc(proj_ready.sem, 1)

            def turn_k(b, i, h):
                if h == 0:
                    pe.wait_ge(k_formed.sem, count(k_formed, b, i + 1))
                pe.wait_ge(kt_drained.sem, count(kt_drained, b, 2 * i if own_bank(b, i) else 2 * i + h))
                for t in range(NT // 2):
                    j = h * NT // 2 + t
                    last = nc.tensor.transpose(kt_bank(b, i, h)[:, t * P:(t + 1) * P], a_row[:, i % 2, j * P:(j + 1) * P], ident[:])
                last.then_inc(kt_ready.sem, 1)

            def out_row(b, i):
                pe.wait_ge(out_drained.sem, count(out_drained, b, i))
                for j in range(NT):
                    if j % (NT // 2) == 0:
                        pe.wait_ge(kt_drained.sem, count(kt_drained, b, 2 * i + 1 + j // (NT // 2)))
                        if i == 0:
                            pe.wait_ge(proj_drained.sem, count(proj_drained, b, V_JOB + j + NT // 2))
                    for n, (l, r) in enumerate(((HI, HI), (HI, LO), (LO, HI))):
                        last = nc.tensor.matmul(out_ps[:], kt[:, l, j, :], vo[:, r, j, :],
                                                start=(j == 0 and n == 0), stop=(j == NT - 1 and n == 2))
                last.then_inc(out_ready.sem, 1)

            for n in range(WVO_JOBS + Z_JOBS):
                if n >= 2:
                    pe.wait_ge(proj_drained.sem, n - 1)
                what, i = setup_jobs[n]
                if n == 0:
                    pe.wait_ge(x_lo.sem, DC)
                    pe.wait_ge(w_lo.sem, 1)
                if what == "wvo":
                    if i == 0:
                        pe.wait_ge(w_lo.sem, 4)
                    three_passes(proj[:, n % 2, :], lambda a, c: wv_s[:, a, c, i * P:(i + 1) * P],
                                 lambda a, c: wo_s[:, a, c, :], DC, proj_ready)
                else:
                    k, c, h = z_jobs[i]
                    w = (wl, wg)[k]
                    three_passes(proj[:, n % 2, :], lambda a, d: w[:, a, d, c * P:(c + 1) * P],
                                 lambda a, d: xs[:, a, d, h * BANK:(h + 1) * BANK], DC, proj_ready)
            pe.wait_ge(ident_ready.sem, 1)

            def batch(b, more):
                pe.wait_ge(proj_drained.sem, count(proj_drained, b, 0))
                diagonal(b, 1)
                diagonal(b, 0)
                for i in range(NT + 1):
                    before, after = jobs(i, more)
                    if i == 0:
                        spread(b, BCAST_G, nsq, nsq_ready)
                    else:
                        turn_k(b, i - 1, 0)
                    if i < NT:
                        gram_row(b, i, 1)
                    if i == 0:
                        spread(b, BCAST_L, rn, rn_ready)
                    run_jobs(b, before)
                    if i > 0:
                        turn_k(b, i - 1, 1)
                    if i < NT:
                        gram_row(b, i, 0)
                    run_jobs(b, after)
                    if i > 0:
                        out_row(b, i - 1)

            pe.wait_ge(w_lo.sem, 5)
            with pe.Fori(0, LAST) as b:
                batch(b, True)
            batch(LAST, False)

        @block.scalar
        def _(act):
            def split_hi(n):
                act.wait_ge(w_scale_ready.sem, (1, 2, 2, 2, 3)[n])
                nc.scalar.activation(split_of(w_split[n], HI), w32[n], ACT.Identity,
                                     scale=wscale[:, n:n + 1]).then_inc(w_hi.sem, 1)

            def x_chunk(c):
                nc.scalar.activation(xs[:, HI, c, :], xT32[:, c, :], ACT.Identity,
                                     scale=sx[:, 0:1]).then_inc(x_hi.sem, 1)

            def z_hi(q, slot_):
                k, c, h = z_jobs[q]
                nc.scalar.copy(z[k][:, HI, c, h * BANK:(h + 1) * BANK], proj[:, slot_, :]).then_inc(proj_hi.sem, 1)

            act.wait_ge(x_scale_ready.sem, 1)
            for c in range(DC):
                x_chunk(c)
            split_hi(0)
            for n, (what, i) in enumerate(setup_jobs):
                if what == "z":
                    act.wait_ge(proj_ready.sem, n + 1)
                    z_hi(i, n % 2)
                if n in (2, 3, 4):
                    split_hi(n - 1)
                if n == 5:
                    act.wait_ge(scalars_loaded.sem, 2 * DMA)
                    nc.scalar.activation(gtmp[:, 0:1], gate[:], ACT.Exp, scale=-1.0)
                    nc.scalar.activation(gtmp[:, 1:2], lsig[:], ACT.Exp).then_inc(scalars_exp.sem, 1)
                if n == WVO_JOBS + Z_JOBS // 2 + 2:
                    split_hi(4)

            def run_jobs(b, todo):
                for job in todo:
                    n = ring_index(job)
                    act.wait_ge(proj_ready.sem, count(proj_ready, b, n + 1))
                    if job[0] == "v":
                        nc.scalar.copy(vo[:, HI, job[1], :], proj[:, n % 2, :]).then_inc(proj_hi.sem, 1)
                    else:
                        z_hi(job[1], n % 2)

            def save_row(b, i, k):
                act.wait_ge(gram_drained[k].sem, count(gram_drained[k], b, i + 2))
                s = slot(i, i + 1)
                nc.scalar.copy(saved[k][:, s:s + NT - 1 - i, :].rearrange("p s q -> p (s q)"),
                               gram[k][:, (i + 1) * P:]).then_inc(gram_saved[k].sem, 1)

            def turned(b, i, h):
                act.wait_ge(kt_ready.sem, count(kt_ready, b, 2 * i + h + 1))
                nc.scalar.copy(kt[:, HI, h * NT // 2:(h + 1) * NT // 2, :].rearrange("p t q -> p (t q)"),
                               kt_bank(b, i, h)).then_inc(kt_hi.sem, 1)

            def normalise(b, i):
                act.wait_ge(ln_ready.sem, count(ln_ready, b, i + 1))
                s = i % 2
                nc.scalar.activation(xy[:, s, :], xy[:, s, :], ACT.Identity, scale=lnp[:, s, 1:2],
                                     bias=lnp[:, s, 2:3]).then_inc(y_ready.sem, 1)

            def batch(b, more):
                for k in (1, 0):
                    act.wait_ge(gram_drained[k].sem, count(gram_drained[k], b, 1))
                    nc.scalar.copy(saved[k][:, DIAG:DIAG + NT, :].rearrange("p s q -> p (s q)"),
                                   gram[k][:]).then_inc(gram_saved[k].sem, 1)
                for i in range(NT + 1):
                    before, after = jobs(i, more)
                    if i > 0:
                        turned(b, i - 1, 0)
                    if more and i in (2, 3):
                        if i == 2:
                            act.wait_ge(x_scale_ready.sem, count(x_scale_ready, b, 1))
                            act.wait_ge(proj_ready.sem, count(proj_ready, b, Z_JOB))
                        x_chunk(2 * i - 4)
                    if i < NT:
                        act.wait_ge(gram_drained[1].sem, count(gram_drained[1], b, i + 2))
                        nc.scalar.activation(e_row[:, i % 2, :], e_row[:, i % 2, :], ACT.Exp,
                                             scale=bc[:, 3:4]).then_inc(exp_done.sem, 1)
                    if i < NT - 1:
                        save_row(b, i, 1)
                    run_jobs(b, before)
                    if i > 0:
                        turned(b, i - 1, 1)
                    if i < NT:
                        act.wait_ge(coef_g_ready.sem, count(coef_g_ready, b, i + 1))
                        nc.scalar.activation(e_row[:, i % 2, :], e_row[:, i % 2, :], ACT.Identity,
                                             scale=coef[:, i % 2, 1:2]).then_inc(e_scaled.sem, 1)
                    if more and i in (2, 3):
                        x_chunk(2 * i - 3)
                    if i > 1:
                        normalise(b, i - 2)
                    if i < NT - 1:
                        save_row(b, i, 0)
                    run_jobs(b, after)
                normalise(b, NT - 1)

            with act.Fori(0, LAST) as b:
                batch(b, True)
            batch(LAST, False)

        @block.vector
        def _(dve):
            links = [0]

            def link(ins, base):
                links[0] += 1
                ins.then_inc(vec_link.sem, 1)
                dve.wait_ge(vec_link.sem, base + links[0])

            def scale_from(out, top, tmp, base):
                link(nc.vector.tensor_scalar(tmp, top, 1e-30, None, ALU.max), base)
                link(nc.vector.tensor_scalar(tmp.bitcast(U32), tmp.bitcast(U32), EXPONENT, None, ALU.bitwise_and), base)
                link(nc.vector.reciprocal(tmp, tmp), base)
                return nc.vector.tensor_scalar(out, tmp, 4.0, None, ALU.mult)

            def top_of(out, in_):
                return nc.vector.tensor_reduce(out, in_, AX_X, ALU.max, apply_absolute_value=True)

            def split_lo(n):
                dve.wait_ge(w_hi.sem, n + 1)
                nc.vector.scalar_tensor_tensor(split_of(w_split[n], LO), w32[n], wscale[:, n:n + 1],
                                               split_of(w_split[n], HI), ALU.mult, ALU.subtract).then_inc(w_lo.sem, 1)

            def weight_top(n):
                dve.wait_ge(w_loaded[n].sem, DMA)
                return top_of(wmax[:, n:n + 1], w32[n])

            def x_chunk(c, value):
                dve.wait_ge(x_hi.sem, value)
                nc.vector.scalar_tensor_tensor(xs[:, LO, c, :], xT32[:, c, :], sx[:, 0:1], xs[:, HI, c, :],
                                               ALU.mult, ALU.subtract).then_inc(x_lo.sem, 1)

            def z_lo(q, s):
                k, c, h = z_jobs[q]
                cols = slice(h * BANK, (h + 1) * BANK)
                nc.vector.tensor_tensor(z[k][:, LO, c, cols], proj[:, s, :], z[k][:, HI, c, cols],
                                        ALU.subtract).then_inc(proj_drained.sem, 1)

            for s in (gram_drained[0], gram_drained[1], kt_drained, out_drained):
                dve.sem_inc(s.sem, 1)
            for c in range(DC):
                dve.wait_ge(first_xT_loaded[c].sem, DMA)
                last = top_of(xmax[:, c:c + 1], xT32[:, c, :])
            link(last, 0)
            nc.vector.tensor_reduce(xmax[:, DC:DC + 1], xmax[:, 0:DC], AX_X, ALU.max).then_inc(x_part.sem, 1)
            weight_top(0).then_inc(w_part.sem, 1)
            dve.wait_ge(x_max_ready.sem, 1)
            scale_from(sx[:, 0:1], xmax[:, DC + 1:DC + 2], sx[:, 1:2], 0).then_inc(x_scale_ready.sem, 1)
            dve.wait_ge(w_max_ready.sem, 1)
            scale_from(wscale[:, 0:1], wtop[:, 0:1], wtmp[:, 0:1], 0).then_inc(w_scale_ready.sem, 1)
            for c in range(DC):
                x_chunk(c, c + 1)
            split_lo(0)
            zs = 0
            for n, (what, i) in enumerate(setup_jobs):
                if n < 3:
                    last = weight_top(n + 1)
                    if n == 2:
                        last.then_inc(w_part.sem, 1)
                if what == "z":
                    zs += 1
                    dve.wait_ge(proj_hi.sem, zs)
                    z_lo(i, n % 2)
                else:
                    dve.wait_ge(proj_ready.sem, n + 1)
                    nc.vector.tensor_copy(wvo32[:, i * D:(i + 1) * D], proj[:, n % 2, :]).then_inc(proj_drained.sem, 1)
                if n == 2:
                    dve.wait_ge(w_max_ready.sem, 2)
                    scale_from(wscale[:, 1:4], wtop[:, 1:4], wtmp[:, 1:4], 0).then_inc(w_scale_ready.sem, 1)
                if n in (3, 4, 5):
                    split_lo(n - 2)
                if n == Z_JOBS // 2:
                    dve.wait_ge(scalars_exp.sem, 1)
                    nc.vector.tensor_tensor(gtmp[:, 3:4], gtmp[:, 1:2], gtmp[:, 1:2], ALU.mult)
                    link(nc.vector.tensor_scalar(gtmp[:, 2:3], gtmp[:, 0:1], 1.0, None, ALU.add), 0)
                    link(nc.vector.reciprocal(gtmp[:, 2:4], gtmp[:, 2:4]), 0)
                    nc.vector.tensor_scalar(fixed[:, 0:1], gtmp[:, 2:3], K_SCALE, None, ALU.mult)
                    nc.vector.tensor_scalar(fixed[:, 1:2], gtmp[:, 2:3], -K_SCALE, K_SCALE, ALU.mult, ALU.add)
                    link(nc.vector.tensor_copy(fixed[:, 2:3], gtmp[:, 3:4]), 0)
                if n == WVO_JOBS + Z_JOBS // 2:
                    dve.wait_ge(proj_drained.sem, WVO_JOBS + Z_JOBS // 2)
                    top_of(wmax[:, 4:5], wvo32).then_inc(w_part.sem, 1)
                if n == WVO_JOBS + Z_JOBS // 2 + 1:
                    dve.wait_ge(w_max_ready.sem, 3)
                    scale_from(wscale[:, 4:5], wtop[:, 4:5], wtmp[:, 4:5], 0).then_inc(w_scale_ready.sem, 1)
                    dve.wait_ge(w_scale_ready.sem, 3)
                    link(nc.vector.tensor_scalar(wtmp[:, 5:6], wscale[:, 4:5], wscale[:, 2:3], wscale[:, 3:4],
                                                 ALU.mult, ALU.mult), 0)
                    link(nc.vector.tensor_copy(fixed[:, 3:4], wtmp[:, 5:6]), 0)
                if n == WVO_JOBS + Z_JOBS // 2 + 3:
                    split_lo(4)
            assert links[0] == VEC_SETUP, links
            dve.wait_ge(w_lo.sem, 5)
            dve.wait_ge(ident_ready.sem, 1)
            dve.wait_ge(mask_ready.sem, 1)

            def run_jobs(b, todo):
                for job in todo:
                    n = ring_index(job)
                    dve.wait_ge(proj_hi.sem, count(proj_hi, b, n - V_JOB + 1))
                    if job[0] == "v":
                        t = job[1]
                        nc.vector.tensor_tensor(vo[:, LO, t, :], proj[:, n % 2, :], vo[:, HI, t, :],
                                                ALU.subtract).then_inc(proj_drained.sem, 1)
                    else:
                        z_lo(job[1], n % 2)

            def squares(b, k, done):
                dve.wait_ge(gram_ready[k].sem, count(gram_ready[k], b, 1))
                prod = e_row[:, k, :].rearrange("p (t q) -> p t q", t=NT)
                eye = ident[:].unsqueeze(1).broadcast_to([P, NT, P])
                nc.vector.tensor_tensor(prod, gram[k][:].rearrange("p (t q) -> p t q", t=NT), eye,
                                        ALU.mult).then_inc(gram_drained[k].sem, 1)
                dve.wait_ge(gram_drained[k].sem, count(gram_drained[k], b, 1))
                last = nc.vector.tensor_reduce(sq[:, k, :], prod, AX_X, ALU.add)
                if done is not None:
                    last.then_inc(done.sem, 1)
                return last

            def unspread(b, first, to):
                for h in range(HALVES):
                    n = first + h
                    dve.wait_ge(proj_ready.sem, count(proj_ready, b, n + 1))
                    nc.vector.tensor_copy(to[:, h * BANK:(h + 1) * BANK], proj[:, n % 2, :]).then_inc(proj_drained.sem, 1)

            def turned(b, i, h):
                dve.wait_ge(kt_hi.sem, count(kt_hi, b, 2 * i + h + 1))
                part = lambda s: kt[:, s, h * NT // 2:(h + 1) * NT // 2, :].rearrange("p t q -> p (t q)")
                nc.vector.tensor_tensor(part(LO), kt_bank(b, i, h), part(HI), ALU.subtract).then_inc(kt_drained.sem, 1)

            def residual(b, i, base):
                s = i % 2
                dve.wait_ge(out_ready.sem, count(out_ready, b, i + 1))
                dve.wait_ge(x_loaded[s].sem, count(x_loaded[s], b, x_wait(i)))
                nc.vector.scalar_tensor_tensor(xy[:, s, :], out_ps[:], bc[:, 4:5], xy[:, s, :],
                                               ALU.mult, ALU.add).then_inc(out_drained.sem, 1)
                dve.wait_ge(out_drained.sem, count(out_drained, b, i + 1))
                links[0] += 1
                nc.vector.bn_stats(stats[:], xy[:, s, :]).then_inc(vec_link.sem, 1)
                hold(dve, vec_link, base + links[0])
                nc.vector.bn_aggr(mv[:, s, :], stats[:]).then_inc(mv_ready.sem, 1)

            def batch(b, more):
                base = count(vec_link, b, 0)
                links[0] = 0
                link(squares(b, 1, None), base)
                nc.vector.tensor_scalar(nsq[:], sq[:, 1, :], -0.5, None, ALU.mult).then_inc(nsq_ready.sem, 1)
                nc.vector.tensor_tensor(bc[:, 0:1], sx[:, 0:1], wscale[:, 0:1], ALU.mult)
                nc.vector.tensor_tensor(bc[:, 1:2], sx[:, 0:1], wscale[:, 1:2], ALU.mult)
                link(nc.vector.tensor_tensor(bc[:, 2:3], sx[:, 0:1], fixed[:, 3:4], ALU.mult), base)
                nc.vector.tensor_scalar(bc[:, 5:6], bc[:, 0:1], EPS, None, ALU.mult)
                link(nc.vector.reciprocal(bc[:, 6:8], bc[:, 1:3]), base)
                nc.vector.tensor_scalar(bc[:, 4:5], bc[:, 7:8], 1.0 / K_SCALE, None, ALU.mult)
                nc.vector.tensor_scalar(bc[:, 3:4], bc[:, 6:7], bc[:, 6:7], fixed[:, 2:3],
                                        ALU.mult, ALU.mult)
                dve.wait_ge(nsq_ready.sem, count(nsq_ready, b, 1))
                squares(b, 0, sq_ready)
                unspread(b, BCAST_G, nsq_b)
                dve.wait_ge(norm_ready.sem, count(norm_ready, b, 1))
                link(nc.vector.tensor_scalar(norm[:], norm[:], bc[:, 5:6], None, ALU.max), base)
                nc.vector.reciprocal(rn[:], norm[:]).then_inc(rn_ready.sem, 1)
                dve.wait_ge(rn_ready.sem, count(rn_ready, b, 1))
                dve.wait_ge(proj_drained.sem, count(proj_drained, b, BCAST_G + HALVES))

                for i in range(NT + 1):
                    s = i % 2
                    before, after = jobs(i, more)
                    if more and i == 2:
                        dve.wait_ge(x_max_ready.sem, count(x_max_ready, b, 1))
                        scale_from(sx[:, 0:1], xmax[:, DC + 1:DC + 2], sx[:, 1:2], base).then_inc(x_scale_ready.sem, 1)
                    if i > 0:
                        turned(b, i - 1, 0)
                    if i > 1:
                        residual(b, i - 2, base)
                    if i < NT:
                        dve.wait_ge(gram_ready[1].sem, count(gram_ready[1], b, i + 2))
                        nc.vector.scalar_tensor_tensor(e_row[:, s, :], gram[1][:], nsq[:, i:i + 1], nsq_b[:],
                                                       ALU.add, ALU.add).then_inc(gram_drained[1].sem, 1)
                    if i == 0:
                        unspread(b, BCAST_L, rn_b)
                    if more and i in (2, 3):
                        x_chunk(2 * i - 4, count(x_hi, b, 2 * i - 3))
                    if i > 0 and turn_early(i, more):
                        turned(b, i - 1, 1)
                    if i < NT:
                        dve.wait_ge(exp_done.sem, count(exp_done, b, i + 1))
                        link(nc.vector.scalar_tensor_tensor(e_row[:, s, :], e_row[:, s, :], 1.0, mask[:, i, :],
                                                            ALU.min, ALU.mult, accum_out=deg[:, s, 1:2]), base)
                        link(nc.vector.tensor_scalar(dinv[:, s, 1:2], deg[:, s, 1:2], EPS, None, ALU.max), base)
                        link(nc.vector.reciprocal(dinv[:, s, 1:2], dinv[:, s, 1:2]), base)
                        nc.vector.tensor_scalar(coef[:, s, 1:2], dinv[:, s, 1:2], fixed[:, 1:2], None,
                                                ALU.mult).then_inc(coef_g_ready.sem, 1)
                    run_jobs(b, before)
                    if i > 0 and not turn_early(i, more):
                        turned(b, i - 1, 1)
                    if i < NT:
                        dve.wait_ge(rmask_ready.sem, count(rmask_ready, b, i + 1))
                        dve.wait_ge(gram_ready[0].sem, count(gram_ready[0], b, i + 2))
                        nc.vector.scalar_tensor_tensor(a_row[:, s, :], gram[0][:], 0.0, rmask[:], ALU.max, ALU.mult,
                                                       accum_out=deg[:, s, 0:1]).then_inc(gram_drained[0].sem, 1)
                        dve.wait_ge(gram_drained[0].sem, count(gram_drained[0], b, i + 2))
                        link(nc.vector.tensor_scalar(dinv[:, s, 0:1], deg[:, s, 0:1], rn[:, i:i + 1], EPS,
                                                     ALU.mult, ALU.max), base)
                        link(nc.vector.reciprocal(dinv[:, s, 0:1], dinv[:, s, 0:1]), base)
                        link(nc.vector.tensor_scalar(coef[:, s, 0:1], dinv[:, s, 0:1], rn[:, i:i + 1], fixed[:, 0:1],
                                                     ALU.mult, ALU.mult), base)
                        dve.wait_ge(e_scaled.sem, count(e_scaled, b, i + 1))
                        nc.vector.scalar_tensor_tensor(a_row[:, s, :], a_row[:, s, :], coef[:, s, 0:1], e_row[:, s, :],
                                                       ALU.mult, ALU.add).then_inc(k_formed.sem, 1)
                    run_jobs(b, after)
                    if more and i in (0, 1):
                        if i == 0:
                            dve.wait_ge(xT_loaded.sem, count(xT_loaded, b, DMA))
                        part = slice(i * DC // 2, (i + 1) * DC // 2)
                        last = top_of(xmax[:, part], xT32[:, part, :])
                        if i == 1:
                            link(last, base)
                            nc.vector.tensor_reduce(xmax[:, DC:DC + 1], xmax[:, 0:DC], AX_X,
                                                    ALU.max).then_inc(x_part.sem, 1)
                    if more and i in (2, 3):
                        x_chunk(2 * i - 3, count(x_hi, b, 2 * i - 2))
                residual(b, NT - 1, base)
                return links[0]

            with dve.Fori(0, LAST) as b:
                used = batch(b, True)
            assert used == vec_link.per_batch, used
            batch(LAST, False)

        @block.gpsimd
        def _(pool):
            nc.gpsimd.memset(ident[:], 0.0).then_inc(ident_zero.sem, 1)
            nc.gpsimd.memset(half[:], 0.5)
            nc.gpsimd.memset(mhalf[:], -0.5).then_inc(halves_ready.sem, 1)
            pool.wait_ge(ident_zero.sem, 1)
            nc.gpsimd.affine_select(out=ident[:], in_=ident[:], compare_op=ALU.not_equal, fill=1.0, base=0,
                                    pattern=[[-1, P]], channel_multiplier=1).then_inc(ident_ready.sem, 1)
            pool.wait_ge(x_part.sem, 1)
            nc.gpsimd.partition_all_reduce(xmax[:, DC + 1:DC + 2], xmax[:, DC:DC + 1], P, RMAX).then_inc(x_max_ready.sem, 1)
            for n, cols in enumerate((slice(0, 1), slice(1, 4), slice(4, 5))):
                if n == 2:
                    pool.wait_ge(mask_loaded.sem, DMA)
                    for t in range(NT):
                        tile = mask[:, t, t * P:(t + 1) * P]
                        last = nc.gpsimd.affine_select(out=tile, in_=tile, compare_op=ALU.not_equal, fill=0.0, base=0,
                                                       pattern=[[-1, P]], channel_multiplier=1)
                    last.then_inc(mask_ready.sem, 1)
                pool.wait_ge(w_part.sem, n + 1)
                nc.gpsimd.partition_all_reduce(wtop[:, cols], wmax[:, cols], P, RMAX).then_inc(w_max_ready.sem, 1)
            pool.wait_ge(halves_ready.sem, 1)
            pool.wait_ge(mask_ready.sem, 1)

            def masked_norms(b, i):
                if i == 0:
                    pool.wait_ge(proj_drained.sem, count(proj_drained, b, BCAST_L + HALVES))
                pool.wait_ge(gram_drained[0].sem, count(gram_drained[0], b, i + 1))
                nc.gpsimd.tensor_tensor(rmask[:], mask[:, i, :], rn_b[:], ALU.mult).then_inc(rmask_ready.sem, 1)

            def layer_norm(b, i):
                s = i % 2
                hold(pool, mv_ready, count(mv_ready, b, i + 1))
                nc.gpsimd.tensor_scalar(lnp[:, s, 0:1], mv[:, s, 1:2], LN_EPS, 1.0, ALU.add,
                                        ALU.mult).then_inc(pool_link.sem, 1)
                pool.wait_ge(pool_link.sem, count(pool_link, b, 2 * i + 1))
                nc.gpsimd.tensor_tensor(lnp[:, s, 1:2], lnp[:, s, 0:1], mhalf[:], ALU.pow).then_inc(pool_link.sem, 1)
                hold(pool, pool_link, count(pool_link, b, 2 * i + 2))
                nc.gpsimd.tensor_scalar(lnp[:, s, 2:3], mv[:, s, 0:1], lnp[:, s, 1:2], -1.0, ALU.mult,
                                        ALU.mult).then_inc(ln_ready.sem, 1)

            def batch(b, more):
                pool.wait_ge(sq_ready.sem, count(sq_ready, b, 1))
                nc.gpsimd.tensor_tensor(norm[:], sq[:, 0, :], half[:], ALU.pow).then_inc(norm_ready.sem, 1)
                masked_norms(b, 0)
                for i in range(NT + 1):
                    if more and i == 2:
                        hold(pool, x_part, count(x_part, b, 1))
                        nc.gpsimd.partition_all_reduce(xmax[:, DC + 1:DC + 2], xmax[:, DC:DC + 1], P,
                                                       RMAX).then_inc(x_max_ready.sem, 1)
                    if i > 1:
                        layer_norm(b, i - 2)
                    if i + 1 < NT:
                        masked_norms(b, i + 1)
                layer_norm(b, NT - 1)

            with pool.Fori(0, LAST) as b:
                batch(b, True)
            batch(LAST, False)


def kernel(x, adj, L0_gnn_W_lang, L0_gnn_W_grav, L0_gnn_W_V, L0_gnn_W_O, L0_gnn_gate_logit, L0_gnn_log_sigma):
    import numpy as np
    import concourse.bacc as bacc
    from concourse.bass_utils import run_bass_kernel_spmd

    x = np.asarray(x)
    arrays = {
        "x": np.ascontiguousarray(x),
        "xT": np.ascontiguousarray(x.transpose(0, 2, 1)),
        "adj": np.ascontiguousarray(adj),
        "WlT": np.ascontiguousarray(np.asarray(L0_gnn_W_lang).T),
        "WgT": np.ascontiguousarray(np.asarray(L0_gnn_W_grav).T),
        "Wv": np.ascontiguousarray(L0_gnn_W_V),
        "WoT": np.ascontiguousarray(np.asarray(L0_gnn_W_O).T),
        "gate_logit": np.asarray(L0_gnn_gate_logit).reshape(1, 1),
        "log_sigma": np.asarray(L0_gnn_log_sigma).reshape(1, 1),
    }
    nc = bacc.Bacc("TRN2", target_bir_lowering=False, num_devices=1)
    args = [nc.dram_tensor(n, a.shape, mybir.dt.from_np(a.dtype), kind="ExternalInput").ap() for n, a in arrays.items()]
    out = nc.dram_tensor("y", x.shape, F32, kind="ExternalOutput").ap()
    program(nc, *args, out)
    r = run_bass_kernel_spmd(nc, [arrays], core_ids=[0])
    return r.results[0]["y"]
```

```python
from collections import namedtuple
from contextlib import ExitStack

import concourse.bass as bass
from concourse import mybir

P = 128
F32 = mybir.dt.float32
F16 = mybir.dt.float16
U32 = mybir.dt.uint32
ALU = mybir.AluOpType
ACT = mybir.ActivationFunctionType
AX_X = mybir.AxisListType.X
RMAX = bass.bass_isa.ReduceOp.max

EPS = 1e-8
LN_EPS = 1e-5
K_SCALE = 2.0 ** 13
EXPONENT = 0x7F800000
BANK = 512
WARM_UP = 19
HI, LO = 0, 1

Signal = namedtuple("Signal", "sem per_batch before")


def count(signal, b, n):
    assert signal.before + n > 0
    return b * signal.per_batch + (signal.before + n)


def program(nc, x, xT, adj, WlT, WgT, Wv, WoT, gate_logit, log_sigma, y):
    B, N, D = x.shape
    NT = N // P
    DC = D // P
    HALVES = N // BANK
    LAST = B - 1
    DMA = 16

    KEPT = NT // 2
    row_base = [sum(NT - 1 - r for r in range(i)) for i in range(KEPT + 1)]
    DIAG = row_base[KEPT]
    SLOTS = DIAG + NT

    def slot(i, j):
        return DIAG + i if i == j else row_base[i % KEPT] + j - i - 1

    BCAST_G, BCAST_L = 0, HALVES
    V_JOB = 2 * HALVES
    Z_JOB = V_JOB + NT
    Z_JOBS = 2 * DC * HALVES
    PROJ_JOBS = Z_JOB + Z_JOBS
    z_jobs = [(k, c, h) for h in range(HALVES) for k in range(2) for c in range(DC)]
    WVO_JOBS = DC
    of_kind = [[("z", q) for q, job in enumerate(z_jobs) if job[0] == k] for k in range(2)]
    WG_FROM = len(of_kind[0])
    WVO_FROM = WG_FROM + 3
    WVO_END = WVO_FROM + WVO_JOBS
    setup_jobs = of_kind[0] + of_kind[1][:3] + [("wvo", i) for i in range(WVO_JOBS)] + of_kind[1][3:]
    all_d, all_e = slice(0, DC), slice(0, D)
    w_pieces = [(0, all_d, slice(c * P, (c + 1) * P)) for c in range(DC)]
    w_pieces += [(n, slice(c, c + 2), all_e) for n in (1, 2, 3) for c in range(0, DC, 2)]
    w_pieces.append((4, all_d, all_e))
    pieces_after = {5: [4, 5], 6: [6, 7], 7: [8], 8: [9], WVO_END + 2: [10]}
    pieces_of = lambda n: 1 + max(p for p in range(len(w_pieces)) if w_pieces[p][0] == n)

    def jobs(i, more):
        first, last = [(0, NT // 2), (NT // 2, NT), (0, 0), (0, 0)][i] if i < KEPT else (
            (2 * (i - KEPT), 2 * (i - KEPT) + 2) if i < NT else (Z_JOBS // 2, Z_JOBS))
        todo = [("v" if i < KEPT else "z", q) for q in range(first, last) if i < KEPT or more]
        mid = 0 if i < KEPT else 1 if i < NT else 2
        return todo[:mid], todo[mid:]

    def early(i, more):
        return not more and i >= 3

    def xy_of(i):
        return 2 if i == NT - 1 else i % 2

    rows_of = [sum(xy_of(i) == s for i in range(NT)) for s in range(3)]

    def ring_index(job):
        return (V_JOB if job[0] == "v" else Z_JOB) + job[1]

    with ExitStack() as ctx:
        def sb(name, shape, dt=F32):
            return ctx.enter_context(nc.sbuf_tensor(name, shape, dt))

        def psum(name, shape):
            return ctx.enter_context(nc.psum_tensor(name, shape, F32))

        def signal(name, per_batch=0, before=0):
            return Signal(ctx.enter_context(nc.semaphore(name)), per_batch, before)

        gram = [psum("gram_l", [P, N]), psum("gram_g", [P, N])]
        proj = psum("proj", [P, 2, BANK])
        kt_ps = psum("kt_ps", [P, BANK])
        out_ps = psum("out_ps", [P, D])

        mask = sb("mask", [P, NT, N])
        wl = sb("wl", [P, 2, DC, D], F16)
        wg = sb("wg", [P, 2, DC, D], F16)
        wvo = sb("wvo", [P, 2, DC, D], F16)
        ident = sb("ident", [P, P])
        xT32 = sb("xT32", [P, DC, N])
        xs = sb("xs", [P, 2, DC, N], F16)
        z = [sb("zl", [P, 2, DC, N], F16), sb("zg", [P, 2, DC, N], F16)]
        vo = sb("vo", [P, 2, NT, D], F16)
        saved = [sb("saved_l", [P, SLOTS, P]), sb("saved_g", [P, SLOTS, P])]
        rn_b = sb("rn_b", [P, N])
        nsq_b = sb("nsq_b", [P, N])
        rmask = sb("rmask", [P, N])
        a_row = sb("a_row", [P, 2, N])
        e_row = sb("e_row", [P, 2, N])
        kt = sb("kt", [P, 2, NT, P], F16)
        xy = sb("xy", [P, 3, D])
        wmax = sb("wmax", [P, 5])
        wtop = sb("wtop", [P, 5])
        wscale = sb("wscale", [P, 5])
        wtmp = sb("wtmp", [P, 6])
        wmax_half = sb("wmax_half", [P, 4, 2])
        gate = sb("gate", [P, 1])
        lsig = sb("lsig", [P, 1])
        gtmp = sb("gtmp", [P, 4])
        fixed = sb("fixed", [P, 4])
        xmax = sb("xmax", [P, DC + 2])
        sx = sb("sx", [P, 4])
        bc = sb("bc", [P, 8])
        sq = sb("sq", [P, 2, NT])
        norm = sb("norm", [P, NT])
        rn = sb("rn", [P, NT])
        nsq = sb("nsq", [P, NT])
        half = sb("half", [P, NT])
        mhalf = sb("mhalf", [P, 1])
        deg = sb("deg", [P, 2, 2])
        dinv = sb("dinv", [P, 2, 2])
        coef = sb("coef", [P, 2, 2])
        stats = sb("stats", [P, 6])
        mv = sb("mv", [P, 3, 2])
        lnp = sb("lnp", [P, 3, 4])

        w_loaded = [[signal(f"w{n}_half{h}_loaded") for h in range(2)] for n in range(4)]
        scalars_loaded = signal("scalars_loaded")
        mask_loaded = signal("mask_loaded")
        first_xT_loaded = [signal(f"first_xT{c}_loaded") for c in range(DC)]
        xT_loaded = signal("xT_loaded", DMA)
        x_loaded = [signal(f"x_loaded{s}", DMA * rows_of[s]) for s in range(3)]
        y_stored = [signal(f"y_stored{s}", DMA * rows_of[s]) for s in range(3)]
        gram_ready = [signal("gram_l_ready", NT + 1), signal("gram_g_ready", NT + 1)]
        proj_ready = signal("proj_ready", PROJ_JOBS, WVO_JOBS + Z_JOBS)
        kt_ready = signal("kt_ready", 2 * NT)
        out_ready = signal("out_ready", NT)
        gram_saved = [signal("gram_l_saved", NT), signal("gram_g_saved", NT)]
        w_hi = signal("w_hi")
        scalars_exp = signal("scalars_exp")
        x_hi = signal("x_hi", DC, DC * HALVES)
        proj_hi = signal("proj_hi", NT + Z_JOBS, Z_JOBS)
        exp_done = signal("exp_done", NT)
        e_scaled = signal("e_scaled", NT)
        kt_hi = signal("kt_hi", 2 * NT)
        y_ready = signal("y_ready", NT)
        gram_drained = [signal("gram_l_drained", NT + 1, 1), signal("gram_g_drained", NT + 1, 1)]
        w_part = signal("w_part")
        w_scale_ready = signal("w_scale_ready")
        w_lo = signal("w_lo")
        x_part = signal("x_part", 1, 1)
        x_scale_ready = signal("x_scale_ready", 1, 1)
        x_lo = signal("x_lo", DC, DC * HALVES)
        sq_ready = signal("sq_ready", 1)
        rn_ready = signal("rn_ready", 1)
        nsq_ready = signal("nsq_ready", 1)
        proj_drained = signal("proj_drained", PROJ_JOBS, WVO_JOBS + Z_JOBS)
        coef_g_ready = signal("coef_g_ready", NT)
        k_formed = signal("k_formed", NT)
        kt_drained = signal("kt_drained", 2 * NT, 1)
        out_drained = signal("out_drained", NT, 1)
        mv_ready = signal("mv_ready", NT)
        VEC_SETUP = 20
        VEC_BATCH = 80
        vec_link = signal("vec_link", VEC_BATCH, VEC_SETUP)
        ident_zero = signal("ident_zero")
        ident_ready = signal("ident_ready")
        mask_ready = signal("mask_ready")
        halves_ready = signal("halves_ready")
        w_max_ready = signal("w_max_ready")
        x_max_ready = signal("x_max_ready", 1, 1)
        norm_ready = signal("norm_ready", 1)
        rmask_ready = signal("rmask_ready", NT)
        ln_ready = signal("ln_ready", NT)
        pool_link = signal("pool_link", 2 * NT)
        passed = signal("passed")

        flat = lambda t, a: t[:].rearrange(a)
        z_half = flat(xT32, "p c n -> p (c n)").bitcast(F16).rearrange("p (k c n) -> p k c n", k=2, c=DC)
        w32 = [
            flat(saved[0], "p s q -> p (s q)")[:, 0:DC * D],
            flat(saved[1], "p s q -> p (s q)")[:, 0:DC * D],
            flat(a_row, "p s n -> p (s n)"),
            flat(vo, "p h t d -> p (h t d)").bitcast(F32)[:, 0:DC * D],
        ]
        wvo32 = flat(e_row, "p s n -> p (s n)")
        w32.append(wvo32)
        in_parts = lambda t: t.rearrange("p (h c e) -> p h c e", h=2, c=DC)
        wv_s = in_parts(flat(saved[0], "p s q -> p (s q)").bitcast(F16)[:, 0:2 * DC * D])
        wo_s = in_parts(flat(vo, "p h t d -> p (h t d)")[:, 2 * DC * D:4 * DC * D])
        w_split = [wl, wg, wv_s, wo_s, wvo]

        def split_of(piece, part):
            n, chunks, cols = w_pieces[piece]
            return w_split[n][:, part, chunks, cols]

        def whole_of(piece):
            n, chunks, cols = w_pieces[piece]
            return w32[n].rearrange("p (c e) -> p c e", c=DC)[:, chunks, cols]

        y_rows = y.rearrange("b (t p) d -> b t p d", p=P)
        x_rows = x.rearrange("b (t p) d -> b t p d", p=P)
        xT_rows = xT.rearrange("b (c p) n -> b p c n", p=P)
        x_wait = lambda i: DMA * sum(xy_of(r) == xy_of(i) for r in range(i + 1))

        block = ctx.enter_context(nc.Block())

        def own_bank(b, i):
            return isinstance(b, int) and early(i + 1, b < LAST)

        def kt_bank(b, i, h):
            return proj[:, 0, :] if h == 1 and own_bank(b, i) else kt_ps[:]

        def hold(eng, signal, value):
            eng.wait_ge(signal.sem, value)
            eng.sem_inc(passed.sem, 1)

        @block.sync
        def _(sp):
            for c in range(DC):
                sp.dma_start(xT32[:, c, :], xT_rows[0][:, c, :]).then_inc(first_xT_loaded[c].sem, DMA)
            for n, src in enumerate((WlT, WgT, Wv, WoT)):
                for h in range(2):
                    chunks = slice(h * DC // 2, (h + 1) * DC // 2)
                    sp.dma_start(w32[n].rearrange("p (c e) -> p c e", c=DC)[:, chunks, :],
                                 src.rearrange("(c p) e -> p c e", p=P)[:, chunks, :]).then_inc(w_loaded[n][h].sem, DMA)
            sp.dma_start(gate[:], gate_logit.broadcast_to([P, 1])).then_inc(scalars_loaded.sem, DMA)
            sp.dma_start(lsig[:], log_sigma.broadcast_to([P, 1])).then_inc(scalars_loaded.sem, DMA)
            sp.dma_start(mask[:], adj.rearrange("(t p) m -> p t m", p=P)).then_inc(mask_loaded.sem, DMA)

            def load_x(b, r):
                sp.dma_start(xy[:, xy_of(r), :], x_rows[b, r]).then_inc(x_loaded[xy_of(r)].sem, DMA)

            def batch(b, more):
                load_x(b, 0)
                load_x(b, 1)
                load_x(b, NT - 1)
                if more:
                    for k in range(2):
                        sp.wait_ge(gram_ready[k].sem, count(gram_ready[k], b, 1))
                    sp.dma_start(xT32[:], xT_rows[b + 1]).then_inc(xT_loaded.sem, DMA)
                for r in range(NT):
                    sp.wait_ge(y_ready.sem, count(y_ready, b, r + 1))
                    sp.dma_start(y_rows[b, r], xy[:, xy_of(r), :]).then_inc(y_stored[xy_of(r)].sem, DMA)
                    if r + 2 < NT - 1:
                        sp.wait_ge(y_stored[xy_of(r)].sem, count(y_stored[xy_of(r)], b, x_wait(r)))
                        load_x(b, r + 2)
                for r in (NT - 3, NT - 2, NT - 1):
                    hold(sp, y_stored[xy_of(r)], count(y_stored[xy_of(r)], b, x_wait(r)))

            with sp.Fori(0, LAST) as b:
                batch(b, True)
            batch(LAST, False)

        @block.tensor
        def _(pe):
            def three_passes(out, left, right, chunks, done, chunk_ready=None):
                passes = [(c, a, b) for c in range(chunks) for a, b in ((HI, HI), (HI, LO), (LO, HI))]
                for n, (c, a, b) in enumerate(passes):
                    if chunk_ready is not None and n % 3 == 0:
                        pe.wait_ge(chunk_ready.sem, c + 1)
                    last = nc.tensor.matmul(out, left(a, c), right(b, c),
                                            start=(n == 0), stop=(n == len(passes) - 1))
                last.then_inc(done.sem, 1)

            def ring_wait(b, n):
                k = count(proj_drained, b, n - 1)
                pe.wait_ge(proj_drained.sem, k)

            def z_job(b, q, n):
                k, c, h = z_jobs[q]
                w = (wl, wg)[k]
                ring_wait(b, n)
                three_passes(proj[:, n % 2, :], lambda a, d: w[:, a, d, c * P:(c + 1) * P],
                             lambda a, d: xs[:, a, d, h * BANK:(h + 1) * BANK], DC, proj_ready)

            def run_jobs(b, todo):
                for job in todo:
                    n = ring_index(job)
                    if job[0] == "v":
                        t = job[1]
                        ring_wait(b, n)
                        three_passes(proj[:, n % 2, :], lambda a, d: xs[:, a, d, t * P:(t + 1) * P],
                                     lambda a, d: wvo[:, a, d, :], DC, proj_ready)
                    else:
                        if job[1] == 0:
                            pe.wait_ge(x_lo.sem, count(x_lo, b, DC))
                        z_job(b, job[1], n)

            def diagonal(b, k):
                pe.wait_ge(gram_drained[k].sem, count(gram_drained[k], b, 0))
                for t in range(NT):
                    if k == 1 and t == NT // 2:
                        pe.wait_ge(proj_drained.sem, count(proj_drained, b, 0))
                    cols = slice(t * P, (t + 1) * P)
                    for c in range(DC):
                        hi = z[k][:, HI, c, cols]
                        nc.tensor.matmul(gram[k][:, cols], hi, z_half[:, k, c, cols], start=(c == 0), stop=False)
                        last = nc.tensor.matmul(gram[k][:, cols], hi, z[k][:, LO, c, cols],
                                                start=False, stop=(c == DC - 1))
                last.then_inc(gram_ready[k].sem, 1)

            def gram_row(b, i, k):
                pe.wait_ge(gram_saved[k].sem, count(gram_saved[k], b, i + 1))
                for j in range(i + 1):
                    last = nc.tensor.transpose(gram[k][:, j * P:(j + 1) * P], saved[k][:, slot(j, i), :], ident[:])
                pieces = [(max((i + 1) * P, h * BANK), (h + 1) * BANK) for h in range(HALVES)]
                pieces = [(a, e) for a, e in pieces if a < e]
                for c in range(DC if pieces else 0):
                    for n, (l, r) in enumerate(((HI, HI), (HI, LO), (LO, HI))):
                        for a, e in pieces:
                            last = nc.tensor.matmul(gram[k][:, a:e], z[k][:, l, c, i * P:(i + 1) * P],
                                                    z[k][:, r, c, a:e], start=(c == 0 and n == 0),
                                                    stop=(c == DC - 1 and n == 2))
                last.then_inc(gram_ready[k].sem, 1)

            def spread(b, first, column, ready):
                pe.wait_ge(ready.sem, count(ready, b, 1))
                for h in range(HALVES):
                    ring_wait(b, first + h)
                    for t in range(BANK // P):
                        col = column[:, h * BANK // P + t:h * BANK // P + t + 1]
                        last = nc.tensor.transpose(proj[:, (first + h) % 2, t * P:(t + 1) * P],
                                                   col.broadcast_to([P, P]), ident[:])
                    last.then_inc(proj_ready.sem, 1)

            def turn_k(b, i, h):
                if h == 0:
                    pe.wait_ge(k_formed.sem, count(k_formed, b, i + 1))
                pe.wait_ge(kt_drained.sem, count(kt_drained, b, 2 * i if own_bank(b, i) else 2 * i + h))
                for t in range(NT // 2):
                    j = h * NT // 2 + t
                    last = nc.tensor.transpose(kt_bank(b, i, h)[:, t * P:(t + 1) * P],
                                               a_row[:, i % 2, j * P:(j + 1) * P], ident[:])
                last.then_inc(kt_ready.sem, 1)

            def out_row(b, i):
                pe.wait_ge(out_drained.sem, count(out_drained, b, i))
                for h in range(2):
                    tiles = range(h * NT // 2, (h + 1) * NT // 2)
                    pe.wait_ge(kt_hi.sem, count(kt_hi, b, 2 * i + 1 + h))
                    if i == 0:
                        pe.wait_ge(proj_drained.sem, count(proj_drained, b, V_JOB + (h + 1) * NT // 2))
                    for j in tiles:
                        for part in (HI, LO):
                            nc.tensor.matmul(out_ps[:], kt[:, HI, j, :], vo[:, part, j, :],
                                             start=(j == 0 and part == HI), stop=False)
                    pe.wait_ge(kt_drained.sem, count(kt_drained, b, 2 * i + 1 + h))
                    for j in tiles:
                        last = nc.tensor.matmul(out_ps[:], kt[:, LO, j, :], vo[:, HI, j, :],
                                                start=False, stop=(j == NT - 1))
                last.then_inc(out_ready.sem, 1)

            pe.wait_ge(ident_ready.sem, 1)
            pe.wait_ge(x_scale_ready.sem, 1)
            for n in range(WARM_UP):
                nc.tensor.transpose(kt_ps[:, n % (NT // 2) * P:(n % (NT // 2) + 1) * P], ident[:], ident[:])

            for n in range(WVO_JOBS + Z_JOBS):
                if n >= 2:
                    pe.wait_ge(proj_drained.sem, n - 1)
                what, i = setup_jobs[n]
                if n < DC:
                    pe.wait_ge(w_lo.sem, n + 1)
                if n == DC:
                    pe.wait_ge(x_lo.sem, DC * HALVES)
                if n == WG_FROM:
                    pe.wait_ge(w_lo.sem, pieces_of(1))
                if what == "wvo":
                    if i == 0:
                        pe.wait_ge(w_lo.sem, pieces_of(3))
                    three_passes(proj[:, n % 2, :], lambda a, c: wv_s[:, a, c, i * P:(i + 1) * P],
                                 lambda a, c: wo_s[:, a, c, :], DC, proj_ready)
                else:
                    k, c, h = z_jobs[i]
                    w = (wl, wg)[k]
                    three_passes(proj[:, n % 2, :], lambda a, d: w[:, a, d, c * P:(c + 1) * P],
                                 lambda a, d: xs[:, a, d, h * BANK:(h + 1) * BANK], DC, proj_ready,
                                 x_lo if n == 0 else None)

            def batch(b, more):
                pe.wait_ge(proj_drained.sem, count(proj_drained, b, -DC))
                diagonal(b, 1)
                diagonal(b, 0)
                for i in range(NT + 1):
                    before, after = jobs(i, more)
                    if i == 0:
                        spread(b, BCAST_G, nsq, nsq_ready)
                    else:
                        turn_k(b, i - 1, 0)
                    if i < NT and not early(i, more):
                        gram_row(b, i, 1)
                    if i == 0:
                        spread(b, BCAST_L, rn, rn_ready)
                    if i == 0:
                        pe.wait_ge(w_lo.sem, pieces_of(4))
                    run_jobs(b, before)
                    if i > 0:
                        turn_k(b, i - 1, 1)
                    if i < NT:
                        gram_row(b, i, 0)
                    if i + 1 < NT and early(i + 1, more):
                        gram_row(b, i + 1, 1)
                    run_jobs(b, after)
                    if i > 0:
                        out_row(b, i - 1)

            with pe.Fori(0, LAST) as b:
                batch(b, True)
            batch(LAST, False)

        @block.scalar
        def _(act):
            def split_hi(piece):
                n = w_pieces[piece][0]
                act.wait_ge(w_scale_ready.sem, (1, 2, 2, 2, 3)[n])
                nc.scalar.activation(split_of(piece, HI), whole_of(piece), ACT.Identity,
                                     scale=wscale[:, n:n + 1]).then_inc(w_hi.sem, 1)

            def x_chunk(c, cols=slice(0, N)):
                nc.scalar.activation(xs[:, HI, c, cols], xT32[:, c, cols], ACT.Identity,
                                     scale=sx[:, 0:1]).then_inc(x_hi.sem, 1)

            def z_hi(q, bank):
                k, c, h = z_jobs[q]
                cols = slice(h * BANK, (h + 1) * BANK)
                nc.scalar.mul(z_half[:, k, c, cols], proj[:, bank, :], 0.5)
                nc.scalar.copy(z[k][:, HI, c, cols], proj[:, bank, :]).then_inc(proj_hi.sem, 1)

            act.wait_ge(x_scale_ready.sem, 1)
            for h in range(HALVES):
                for c in range(DC):
                    x_chunk(c, slice(h * BANK, (h + 1) * BANK))
                if h == 0:
                    for piece in range(DC):
                        split_hi(piece)
            for n, (what, i) in enumerate(setup_jobs):
                if what == "z":
                    act.wait_ge(proj_ready.sem, n + 1)
                    if 1 <= n <= DC:
                        act.wait_ge(x_lo.sem, DC + n)
                    z_hi(i, n % 2)
                for piece in pieces_after.get(n, ()):
                    split_hi(piece)
                if n == WVO_FROM:
                    act.wait_ge(scalars_loaded.sem, 2 * DMA)
                    nc.scalar.activation(gtmp[:, 0:1], gate[:], ACT.Exp, scale=-1.0)
                    nc.scalar.activation(gtmp[:, 1:2], lsig[:], ACT.Exp).then_inc(scalars_exp.sem, 1)

            def run_jobs(b, todo):
                for job in todo:
                    n = ring_index(job)
                    act.wait_ge(proj_ready.sem, count(proj_ready, b, n + 1))
                    if job[0] == "v":
                        nc.scalar.copy(vo[:, HI, job[1], :], proj[:, n % 2, :]).then_inc(proj_hi.sem, 1)
                    else:
                        z_hi(job[1], n % 2)

            def save_row(b, i, k):
                act.wait_ge(gram_drained[k].sem, count(gram_drained[k], b, i + 2))
                s = slot(i, i + 1)
                nc.scalar.copy(saved[k][:, s:s + NT - 1 - i, :].rearrange("p s q -> p (s q)"),
                               gram[k][:, (i + 1) * P:]).then_inc(gram_saved[k].sem, 1)

            def turned(b, i, h):
                act.wait_ge(kt_ready.sem, count(kt_ready, b, 2 * i + h + 1))
                nc.scalar.copy(kt[:, HI, h * NT // 2:(h + 1) * NT // 2, :].rearrange("p t q -> p (t q)"),
                               kt_bank(b, i, h)).then_inc(kt_hi.sem, 1)

            def normalise(b, i):
                act.wait_ge(ln_ready.sem, count(ln_ready, b, i + 1))
                s, xy_row = xy_of(i), xy[:, xy_of(i), :]
                nc.scalar.activation(xy_row, xy_row, ACT.Identity, scale=lnp[:, s, 1:2],
                                     bias=lnp[:, s, 2:3]).then_inc(y_ready.sem, 1)

            def batch(b, more):
                for k in (1, 0):
                    act.wait_ge(gram_drained[k].sem, count(gram_drained[k], b, 1))
                    nc.scalar.copy(saved[k][:, DIAG:DIAG + NT, :].rearrange("p s q -> p (s q)"),
                                   gram[k][:]).then_inc(gram_saved[k].sem, 1)
                for i in range(NT + 1):
                    before, after = jobs(i, more)
                    if i > 0 and not early(i, more):
                        turned(b, i - 1, 0)
                    if more and i in (2, 3):
                        if i == 2:
                            act.wait_ge(x_scale_ready.sem, count(x_scale_ready, b, 1))
                            act.wait_ge(proj_ready.sem, count(proj_ready, b, Z_JOB))
                        x_chunk(2 * i - 4)
                    if early(i, more):
                        turned(b, i - 1, 0)
                        turned(b, i - 1, 1)
                        if i < NT - 1:
                            save_row(b, i, 1)
                    if i < NT:
                        act.wait_ge(gram_drained[1].sem, count(gram_drained[1], b, i + 2))
                        nc.scalar.activation(e_row[:, i % 2, :], e_row[:, i % 2, :], ACT.Exp,
                                             scale=bc[:, 3:4]).then_inc(exp_done.sem, 1)
                    if i < NT - 1 and not early(i, more):
                        save_row(b, i, 1)
                    run_jobs(b, before)
                    if i > 0 and not early(i, more):
                        turned(b, i - 1, 1)
                    if i < NT:
                        act.wait_ge(coef_g_ready.sem, count(coef_g_ready, b, i + 1))
                        nc.scalar.activation(e_row[:, i % 2, :], e_row[:, i % 2, :], ACT.Identity,
                                             scale=coef[:, i % 2, 1:2]).then_inc(e_scaled.sem, 1)
                    if more and i in (2, 3):
                        x_chunk(2 * i - 3)
                    if i == NT and not more:
                        normalise(b, i - 3)
                    if i > 1 and (more or i != NT - 1):
                        normalise(b, i - 2)
                    if i < NT - 1:
                        save_row(b, i, 0)
                    run_jobs(b, after)
                normalise(b, NT - 1)

            with act.Fori(0, LAST) as b:
                batch(b, True)
            batch(LAST, False)

        @block.vector
        def _(dve):
            links = [0]

            def link(ins, base):
                links[0] += 1
                ins.then_inc(vec_link.sem, 1)
                dve.wait_ge(vec_link.sem, base + links[0])

            def scale_from(out, top, tmp, base):
                link(nc.vector.tensor_scalar(tmp, top, 1e-30, None, ALU.max), base)
                link(nc.vector.tensor_scalar(tmp.bitcast(U32), tmp.bitcast(U32), EXPONENT, None, ALU.bitwise_and), base)
                link(nc.vector.reciprocal(tmp, tmp), base)
                return nc.vector.tensor_scalar(out, tmp, 4.0, None, ALU.mult)

            def top_of(out, in_):
                return nc.vector.tensor_reduce(out, in_, AX_X, ALU.max, apply_absolute_value=True)

            def weight_top(n, h):
                dve.wait_ge(w_loaded[n][h].sem, DMA)
                return top_of(wmax_half[:, n, h:h + 1], w32[n][:, h * DC * D // 2:(h + 1) * DC * D // 2])

            def split_lo(piece):
                dve.wait_ge(w_hi.sem, piece + 1)
                n = w_pieces[piece][0]
                nc.vector.scalar_tensor_tensor(split_of(piece, LO), whole_of(piece), wscale[:, n:n + 1],
                                               split_of(piece, HI), ALU.mult, ALU.subtract).then_inc(w_lo.sem, 1)

            def x_chunk(c, value, cols=slice(0, N)):
                dve.wait_ge(x_hi.sem, value)
                nc.vector.scalar_tensor_tensor(xs[:, LO, c, cols], xT32[:, c, cols], sx[:, 0:1], xs[:, HI, c, cols],
                                               ALU.mult, ALU.subtract).then_inc(x_lo.sem, 1)

            def z_lo(q, s):
                k, c, h = z_jobs[q]
                cols = slice(h * BANK, (h + 1) * BANK)
                nc.vector.tensor_tensor(z[k][:, LO, c, cols], proj[:, s, :], z[k][:, HI, c, cols],
                                        ALU.subtract).then_inc(proj_drained.sem, 1)

            for s in (gram_drained[0], gram_drained[1], kt_drained, out_drained):
                dve.sem_inc(s.sem, 1)
            for c in range(DC):
                dve.wait_ge(first_xT_loaded[c].sem, DMA)
                last = top_of(xmax[:, c:c + 1], xT32[:, c, :])
            link(last, 0)
            nc.vector.tensor_reduce(xmax[:, DC:DC + 1], xmax[:, 0:DC], AX_X, ALU.max).then_inc(x_part.sem, 1)
            weight_top(0, 0)
            dve.wait_ge(x_max_ready.sem, 1)
            scale_from(sx[:, 0:1], xmax[:, DC + 1:DC + 2], sx[:, 1:2], 0).then_inc(x_scale_ready.sem, 1)
            link(weight_top(0, 1), 0)
            nc.vector.tensor_reduce(wmax[:, 0:1], wmax_half[:, 0, :], AX_X, ALU.max).then_inc(w_part.sem, 1)
            first_half, second_half = slice(0, BANK), slice(BANK, N)
            x_chunk(0, 1, first_half)
            dve.wait_ge(w_max_ready.sem, 1)
            scale_from(wscale[:, 0:1], wtop[:, 0:1], wtmp[:, 0:1], 0).then_inc(w_scale_ready.sem, 1)
            x_chunk(1, 2, first_half)
            split_lo(0)
            for c in range(2, DC):
                x_chunk(c, c + 1, first_half)
            for c in range(1, DC):
                split_lo(c)
            x_chunk(0, DC + 1, second_half)
            zs = 0
            tops_after = {0: [(1, 0)], 1: [(1, 1)], 2: [(2, 0), (2, 1)], 3: [(3, 0), (3, 1)]}
            x_after = {0: [1], 1: [2, 3]}
            for n, (what, i) in enumerate(setup_jobs):
                if what == "z":
                    zs += 1
                    dve.wait_ge(proj_hi.sem, zs)
                    z_lo(i, n % 2)
                else:
                    dve.wait_ge(proj_ready.sem, n + 1)
                    nc.vector.tensor_copy(wvo32[:, i * D:(i + 1) * D], proj[:, n % 2, :]).then_inc(proj_drained.sem, 1)
                for c in x_after.get(n, ()):
                    x_chunk(c, DC + c + 1, second_half)
                for w, h in tops_after.get(n, ()):
                    last = weight_top(w, h)
                if n == 3:
                    link(last, 0)
                    nc.vector.tensor_reduce(wmax[:, 1:4], wmax_half[:, 1:4, :], AX_X, ALU.max).then_inc(w_part.sem, 1)
                if n == 4:
                    dve.wait_ge(w_max_ready.sem, 2)
                    scale_from(wscale[:, 1:4], wtop[:, 1:4], wtmp[:, 1:4], 0).then_inc(w_scale_ready.sem, 1)
                for piece in pieces_after.get(n, ()) if n < WVO_FROM else ():
                    split_lo(piece)
                if n == WVO_END - 1:
                    dve.wait_ge(scalars_exp.sem, 1)
                    nc.vector.tensor_tensor(gtmp[:, 3:4], gtmp[:, 1:2], gtmp[:, 1:2], ALU.mult)
                    link(nc.vector.tensor_scalar(gtmp[:, 2:3], gtmp[:, 0:1], 1.0, None, ALU.add), 0)
                    link(nc.vector.reciprocal(gtmp[:, 2:4], gtmp[:, 2:4]), 0)
                    nc.vector.tensor_scalar(fixed[:, 0:1], gtmp[:, 2:3], K_SCALE, None, ALU.mult)
                    nc.vector.tensor_scalar(fixed[:, 1:2], gtmp[:, 2:3], -K_SCALE, K_SCALE, ALU.mult, ALU.add)
                    link(nc.vector.tensor_copy(fixed[:, 2:3], gtmp[:, 3:4]), 0)
                if n == WVO_END:
                    dve.wait_ge(proj_drained.sem, WVO_END)
                    top_of(wmax[:, 4:5], wvo32).then_inc(w_part.sem, 1)
                if n == WVO_END + 1:
                    dve.wait_ge(w_max_ready.sem, 3)
                    scale_from(wscale[:, 4:5], wtop[:, 4:5], wtmp[:, 4:5], 0).then_inc(w_scale_ready.sem, 1)
                    dve.wait_ge(w_scale_ready.sem, 3)
                    link(nc.vector.tensor_scalar(wtmp[:, 5:6], wscale[:, 4:5], wscale[:, 2:3], wscale[:, 3:4],
                                                 ALU.mult, ALU.mult), 0)
                    link(nc.vector.tensor_copy(fixed[:, 3:4], wtmp[:, 5:6]), 0)
                if n == WVO_END + 3:
                    split_lo(pieces_of(4) - 1)
            assert links[0] == VEC_SETUP, links
            dve.wait_ge(w_lo.sem, len(w_pieces))
            dve.wait_ge(ident_ready.sem, 1)
            dve.wait_ge(mask_ready.sem, 1)

            def run_jobs(b, todo):
                for job in todo:
                    n = ring_index(job)
                    dve.wait_ge(proj_hi.sem, count(proj_hi, b, n - V_JOB + 1))
                    if job[0] == "v":
                        t = job[1]
                        nc.vector.tensor_tensor(vo[:, LO, t, :], proj[:, n % 2, :], vo[:, HI, t, :],
                                                ALU.subtract).then_inc(proj_drained.sem, 1)
                    else:
                        z_lo(job[1], n % 2)

            def squares(b, k, done):
                dve.wait_ge(gram_ready[k].sem, count(gram_ready[k], b, 1))
                prod = e_row[:, k, :].rearrange("p (t q) -> p t q", t=NT)
                eye = ident[:].unsqueeze(1).broadcast_to([P, NT, P])
                nc.vector.scalar_tensor_tensor(prod, gram[k][:].rearrange("p (t q) -> p t q", t=NT), 2.0, eye,
                                               ALU.mult, ALU.mult).then_inc(gram_drained[k].sem, 1)
                dve.wait_ge(gram_drained[k].sem, count(gram_drained[k], b, 1))
                last = nc.vector.tensor_reduce(sq[:, k, :], prod, AX_X, ALU.add)
                if done is not None:
                    last.then_inc(done.sem, 1)
                return last

            def whole_diagonal(b, i, k, base):
                dve.wait_ge(gram_ready[k].sem, count(gram_ready[k], b, i + 2))
                tile = gram[k][:, i * P:(i + 1) * P]
                link(nc.vector.tensor_tensor(tile, tile, saved[k][:, slot(i, i), :], ALU.add), base)

            def unspread(b, first, to):
                for h in range(HALVES):
                    n = first + h
                    dve.wait_ge(proj_ready.sem, count(proj_ready, b, n + 1))
                    nc.vector.tensor_copy(to[:, h * BANK:(h + 1) * BANK], proj[:, n % 2, :]).then_inc(proj_drained.sem, 1)

            def turned(b, i, h):
                dve.wait_ge(kt_hi.sem, count(kt_hi, b, 2 * i + h + 1))
                part = lambda s: kt[:, s, h * NT // 2:(h + 1) * NT // 2, :].rearrange("p t q -> p (t q)")
                nc.vector.tensor_tensor(part(LO), kt_bank(b, i, h), part(HI), ALU.subtract).then_inc(kt_drained.sem, 1)

            def residual(b, i):
                s = xy_of(i)
                dve.wait_ge(out_ready.sem, count(out_ready, b, i + 1))
                dve.wait_ge(x_loaded[s].sem, count(x_loaded[s], b, x_wait(i)))
                nc.vector.scalar_tensor_tensor(xy[:, s, :], out_ps[:], bc[:, 4:5], xy[:, s, :],
                                               ALU.mult, ALU.add).then_inc(out_drained.sem, 1)

            def moments(b, i, base):
                s = xy_of(i)
                dve.wait_ge(out_drained.sem, count(out_drained, b, i + 1))
                links[0] += 1
                nc.vector.bn_stats(stats[:], xy[:, s, :]).then_inc(vec_link.sem, 1)
                hold(dve, vec_link, base + links[0])
                nc.vector.bn_aggr(mv[:, s, :], stats[:]).then_inc(mv_ready.sem, 1)

            def batch(b, more):
                base = count(vec_link, b, 0)
                links[0] = 0
                link(squares(b, 1, None), base)
                nc.vector.tensor_scalar(nsq[:], sq[:, 1, :], -0.5, None, ALU.mult).then_inc(nsq_ready.sem, 1)
                nc.vector.tensor_tensor(bc[:, 0:1], sx[:, 0:1], wscale[:, 0:1], ALU.mult)
                nc.vector.tensor_tensor(bc[:, 1:2], sx[:, 0:1], wscale[:, 1:2], ALU.mult)
                link(nc.vector.tensor_tensor(bc[:, 2:3], sx[:, 0:1], fixed[:, 3:4], ALU.mult), base)
                nc.vector.tensor_scalar(bc[:, 5:6], bc[:, 0:1], EPS, None, ALU.mult)
                link(nc.vector.reciprocal(bc[:, 6:8], bc[:, 1:3]), base)
                nc.vector.tensor_scalar(bc[:, 4:5], bc[:, 7:8], 1.0 / K_SCALE, None, ALU.mult)
                nc.vector.tensor_scalar(bc[:, 3:4], bc[:, 6:7], bc[:, 6:7], fixed[:, 2:3],
                                        ALU.mult, ALU.mult)
                dve.wait_ge(nsq_ready.sem, count(nsq_ready, b, 1))
                squares(b, 0, sq_ready)
                unspread(b, BCAST_G, nsq_b)
                dve.wait_ge(norm_ready.sem, count(norm_ready, b, 1))
                link(nc.vector.tensor_scalar(norm[:], norm[:], bc[:, 5:6], None, ALU.max), base)
                nc.vector.reciprocal(rn[:], norm[:]).then_inc(rn_ready.sem, 1)
                dve.wait_ge(rn_ready.sem, count(rn_ready, b, 1))
                dve.wait_ge(proj_drained.sem, count(proj_drained, b, BCAST_G + HALVES))

                for i in range(NT + 1):
                    s = i % 2
                    before, after = jobs(i, more)
                    if more and i == 2:
                        dve.wait_ge(x_max_ready.sem, count(x_max_ready, b, 1))
                        scale_from(sx[:, 0:1], xmax[:, DC + 1:DC + 2], sx[:, 1:2], base).then_inc(x_scale_ready.sem, 1)
                    if i > 0 and not early(i, more):
                        turned(b, i - 1, 0)
                    if i > 1 and not early(i, more):
                        residual(b, i - 2)
                        moments(b, i - 2, base)
                    if i < NT:
                        whole_diagonal(b, i, 1, base)
                        nc.vector.scalar_tensor_tensor(e_row[:, s, :], gram[1][:], nsq[:, i:i + 1], nsq_b[:],
                                                       ALU.add, ALU.add).then_inc(gram_drained[1].sem, 1)
                    if i == 0:
                        unspread(b, BCAST_L, rn_b)
                    if more and i in (2, 3):
                        x_chunk(2 * i - 4, count(x_hi, b, 2 * i - 3))
                    if early(i, more):
                        residual(b, i - 2)
                        turned(b, i - 1, 0)
                        turned(b, i - 1, 1)
                        if i < NT - 1 or i == NT:
                            moments(b, i - 2, base)
                    if i < NT:
                        dve.wait_ge(exp_done.sem, count(exp_done, b, i + 1))
                        link(nc.vector.scalar_tensor_tensor(e_row[:, s, :], e_row[:, s, :], 1.0, mask[:, i, :],
                                                            ALU.min, ALU.mult, accum_out=deg[:, s, 1:2]), base)
                        link(nc.vector.tensor_scalar(dinv[:, s, 1:2], deg[:, s, 1:2], EPS, None, ALU.max), base)
                        link(nc.vector.reciprocal(dinv[:, s, 1:2], dinv[:, s, 1:2]), base)
                        nc.vector.tensor_scalar(coef[:, s, 1:2], dinv[:, s, 1:2], fixed[:, 1:2], None,
                                                ALU.mult).then_inc(coef_g_ready.sem, 1)
                    run_jobs(b, before)
                    if i > 0 and not early(i, more):
                        turned(b, i - 1, 1)
                    if i < NT:
                        whole_diagonal(b, i, 0, base)
                        dve.wait_ge(rmask_ready.sem, count(rmask_ready, b, i + 1))
                        nc.vector.scalar_tensor_tensor(a_row[:, s, :], gram[0][:], 0.0, rmask[:], ALU.max, ALU.mult,
                                                       accum_out=deg[:, s, 0:1]).then_inc(gram_drained[0].sem, 1)
                        dve.wait_ge(gram_drained[0].sem, count(gram_drained[0], b, i + 2))
                        link(nc.vector.tensor_scalar(dinv[:, s, 0:1], deg[:, s, 0:1], rn[:, i:i + 1], EPS,
                                                     ALU.mult, ALU.max), base)
                        link(nc.vector.reciprocal(dinv[:, s, 0:1], dinv[:, s, 0:1]), base)
                        link(nc.vector.tensor_scalar(coef[:, s, 0:1], dinv[:, s, 0:1], rn[:, i:i + 1], fixed[:, 0:1],
                                                     ALU.mult, ALU.mult), base)
                        dve.wait_ge(e_scaled.sem, count(e_scaled, b, i + 1))
                        nc.vector.scalar_tensor_tensor(a_row[:, s, :], a_row[:, s, :], coef[:, s, 0:1], e_row[:, s, :],
                                                       ALU.mult, ALU.add).then_inc(k_formed.sem, 1)
                    if not more and i == NT - 1:
                        moments(b, i - 2, base)
                    run_jobs(b, after)
                    if more and i in (0, 1):
                        if i == 0:
                            dve.wait_ge(xT_loaded.sem, count(xT_loaded, b, DMA))
                        part = slice(i * DC // 2, (i + 1) * DC // 2)
                        last = top_of(xmax[:, part], xT32[:, part, :])
                        if i == 1:
                            link(last, base)
                            nc.vector.tensor_reduce(xmax[:, DC:DC + 1], xmax[:, 0:DC], AX_X,
                                                    ALU.max).then_inc(x_part.sem, 1)
                    if more and i in (2, 3):
                        x_chunk(2 * i - 3, count(x_hi, b, 2 * i - 2))
                residual(b, NT - 1)
                moments(b, NT - 1, base)
                return links[0]

            with dve.Fori(0, LAST) as b:
                used = batch(b, True)
            assert used == vec_link.per_batch, used
            batch(LAST, False)

        @block.gpsimd
        def _(pool):
            nc.gpsimd.memset(ident[:], 0.0).then_inc(ident_zero.sem, 1)
            nc.gpsimd.memset(half[:], 0.5)
            nc.gpsimd.memset(mhalf[:], -0.5).then_inc(halves_ready.sem, 1)
            pool.wait_ge(ident_zero.sem, 1)
            nc.gpsimd.affine_select(out=ident[:], in_=ident[:], compare_op=ALU.not_equal, fill=1.0, base=0,
                                    pattern=[[-1, P]], channel_multiplier=1).then_inc(ident_ready.sem, 1)
            pool.wait_ge(x_part.sem, 1)
            nc.gpsimd.partition_all_reduce(xmax[:, DC + 1:DC + 2], xmax[:, DC:DC + 1], P,
                                           RMAX).then_inc(x_max_ready.sem, 1)
            for n, cols in enumerate((slice(0, 1), slice(1, 4), slice(4, 5))):
                if n == 2:
                    pool.wait_ge(mask_loaded.sem, DMA)
                    for t in range(NT):
                        tile = mask[:, t, t * P:(t + 1) * P]
                        last = nc.gpsimd.affine_select(out=tile, in_=tile, compare_op=ALU.not_equal, fill=0.0, base=0,
                                                       pattern=[[-1, P]], channel_multiplier=1)
                    last.then_inc(mask_ready.sem, 1)
                pool.wait_ge(w_part.sem, n + 1)
                nc.gpsimd.partition_all_reduce(wtop[:, cols], wmax[:, cols], P, RMAX).then_inc(w_max_ready.sem, 1)
            pool.wait_ge(halves_ready.sem, 1)
            pool.wait_ge(mask_ready.sem, 1)

            def masked_norms(b, i):
                if i == 0:
                    pool.wait_ge(proj_drained.sem, count(proj_drained, b, BCAST_L + HALVES))
                pool.wait_ge(gram_drained[0].sem, count(gram_drained[0], b, i + 1))
                nc.gpsimd.tensor_tensor(rmask[:], mask[:, i, :], rn_b[:], ALU.mult).then_inc(rmask_ready.sem, 1)

            def layer_norm(b, i):
                s = xy_of(i)
                hold(pool, mv_ready, count(mv_ready, b, i + 1))
                nc.gpsimd.tensor_scalar(lnp[:, s, 0:1], mv[:, s, 1:2], LN_EPS, 1.0, ALU.add,
                                        ALU.mult).then_inc(pool_link.sem, 1)
                pool.wait_ge(pool_link.sem, count(pool_link, b, 2 * i + 1))
                nc.gpsimd.tensor_tensor(lnp[:, s, 1:2], lnp[:, s, 0:1], mhalf[:], ALU.pow).then_inc(pool_link.sem, 1)
                hold(pool, pool_link, count(pool_link, b, 2 * i + 2))
                nc.gpsimd.tensor_scalar(lnp[:, s, 2:3], mv[:, s, 0:1], lnp[:, s, 1:2], -1.0, ALU.mult,
                                        ALU.mult).then_inc(ln_ready.sem, 1)

            def batch(b, more):
                pool.wait_ge(sq_ready.sem, count(sq_ready, b, 1))
                nc.gpsimd.tensor_tensor(norm[:], sq[:, 0, :], half[:], ALU.pow).then_inc(norm_ready.sem, 1)
                masked_norms(b, 0)
                for i in range(NT + 1):
                    if more and i == 2:
                        hold(pool, x_part, count(x_part, b, 1))
                        nc.gpsimd.partition_all_reduce(xmax[:, DC + 1:DC + 2], xmax[:, DC:DC + 1], P,
                                                       RMAX).then_inc(x_max_ready.sem, 1)
                    if i > 1:
                        layer_norm(b, i - 2)
                    if i + 1 < NT:
                        masked_norms(b, i + 1)
                layer_norm(b, NT - 1)

            with pool.Fori(0, LAST) as b:
                batch(b, True)
            batch(LAST, False)


def kernel(x, adj, L0_gnn_W_lang, L0_gnn_W_grav, L0_gnn_W_V, L0_gnn_W_O, L0_gnn_gate_logit, L0_gnn_log_sigma):
    import numpy as np
    import concourse.bacc as bacc
    from concourse.bass_utils import run_bass_kernel_spmd

    x = np.asarray(x)
    arrays = {
        "x": np.ascontiguousarray(x),
        "xT": np.ascontiguousarray(x.transpose(0, 2, 1)),
        "adj": np.ascontiguousarray(adj),
        "WlT": np.ascontiguousarray(np.asarray(L0_gnn_W_lang).T),
        "WgT": np.ascontiguousarray(np.asarray(L0_gnn_W_grav).T),
        "Wv": np.ascontiguousarray(L0_gnn_W_V),
        "WoT": np.ascontiguousarray(np.asarray(L0_gnn_W_O).T),
        "gate_logit": np.asarray(L0_gnn_gate_logit).reshape(1, 1),
        "log_sigma": np.asarray(L0_gnn_log_sigma).reshape(1, 1),
    }
    nc = bacc.Bacc("TRN2", target_bir_lowering=False, num_devices=1)
    args = [nc.dram_tensor(n, a.shape, mybir.dt.from_np(a.dtype), kind="ExternalInput").ap() for n, a in arrays.items()]
    out = nc.dram_tensor("y", x.shape, F32, kind="ExternalOutput").ap()
    program(nc, *args, out)
    r = run_bass_kernel_spmd(nc, [arrays], core_ids=[0])
    return r.results[0]["y"]
```
